# Optimizing a Trainium2 kernel written in Bass

```python
import numpy as np
import jax
import jax.numpy as jnp

def _softmax(x, axis=-1):
    return jax.nn.softmax(x, axis=axis)

def _gelu(x):
    return jax.nn.gelu(x, approximate=True)

def _silu(x):
    return jax.nn.silu(x)

def _sigmoid(x):
    return jax.nn.sigmoid(x)

def _layernorm(x, axis=-1, eps=1e-05):
    m = jnp.mean(x, axis=axis, keepdims=True)
    v = jnp.var(x, axis=axis, keepdims=True)
    return (x - m) / jnp.sqrt(v + eps)

def _scatter_add(tgt, idx, src, axis=0):
    return tgt.at[idx].add(src)

def _segment_sum(src, seg, n):
    return jax.ops.segment_sum(src, seg, n)
kernel_name = 'mk_decoder_preln_d1_seqx_r8_8a3939'

def setup_inputs(seed: int=0):
    np.random.seed(seed)
    _w = jnp.asarray

    def _rec_inputs():
        import jax
        import jax.numpy as jnp
        _rk = jax.random.key(seed)
        x = 7.22e-05 + 1 * jax.random.normal(jax.random.fold_in(_rk, 1), (64, 64, 128), jnp.float32)
        _lenS = 64 - jax.random.randint(jax.random.fold_in(_rk, 7), (64,), 0, max(1, 64 // 4) + 1, jnp.int32)
        _lenS2 = 64 - jax.random.randint(jax.random.fold_in(_rk, 8), (64,), 0, max(1, 64 // 4) + 1, jnp.int32)
        _ctx_1024P = jax.random.normal(jax.random.fold_in(_rk, 11), (64, 16, 128), jnp.float32)
        _ctx_1024c = jax.random.dirichlet(jax.random.fold_in(_rk, 511), 0.3 * jnp.ones((16,), jnp.float32), (64, 64))
        _ctx_1024t = jnp.einsum('bsk,bkd->bsd', _ctx_1024c, _ctx_1024P)
        _ctx_1024t = _ctx_1024t * jax.lax.rsqrt(jnp.mean(jnp.square(_ctx_1024t)) + 1e-12) * 0.953939
        ctx_1024 = 4.13588e-05 + 0.999923 * (_ctx_1024t + 0.3 * jax.random.normal(jax.random.fold_in(_rk, 611), (64, 64, 128), jnp.float32))
        _validS = jnp.arange(64)[None, :] < _lenS[:, None]
        _validS2 = jnp.arange(64)[None, :] < _lenS2[:, None]
        _causal = jnp.tril(jnp.ones((64, 64), dtype=bool))
        mask_1_bf0 = jnp.logical_not(jnp.ones((1,), dtype=bool))
        return (x, ctx_1024, mask_1_bf0)
    x, ctx_1024, mask_1_bf0 = _rec_inputs()

    def _L0_attn_setup():
        import jax, jax.numpy as jnp
        import numpy as np
        NUM_HEADS = 8
        D_CONV = 4
        NORMALIZER = 16.0
        LN_EPS = 1e-05

        def _causal_dwconv_silu(x, w):
            xt = jnp.transpose(x, (0, 2, 1))
            y = jax.lax.conv_general_dilated(xt, w[:, None, :], window_strides=(1,), padding=[(w.shape[1] - 1, 0)], feature_group_count=x.shape[-1], dimension_numbers=('NCH', 'OIH', 'NCH'))
            return jnp.transpose(jax.nn.silu(y), (0, 2, 1))

        def _gla(q, k, v, gk, scale):
            B, H, L, Dk = q.shape
            Dv = v.shape[-1]

            def step(S, inp):
                qt, kt, vt, gt = inp
                S = S * jnp.exp(gt)[..., None] + kt[..., None] * vt[..., None, :]
                ot = jnp.einsum('bhk,bhkv->bhv', qt * scale, S)
                return (S, ot)
            mv = lambda a: jnp.moveaxis(a, 2, 0)
            S0 = jnp.zeros((B, H, Dk, Dv), q.dtype)
            _, o = jax.lax.scan(step, S0, (mv(q), mv(k), mv(v), mv(gk)))
            return jnp.moveaxis(o, 0, 2)
        key = jax.random.key(seed)
        ks = jax.random.split(key, 9)
        B, L, E = (4, 256, 128)
        dk = E // 2
        return {'x': jax.random.normal(ks[0], (B, L, E), jnp.float32), 'conv_w': jax.random.normal(ks[1], (E, D_CONV), jnp.float32) * 0.3, 'wq': jax.random.normal(ks[2], (E, dk), jnp.float32) * 0.02, 'wkg': jax.random.normal(ks[3], (E, dk), jnp.float32) * 0.02, 'wv': jax.random.normal(ks[4], (E, E), jnp.float32) * 0.02, 'wg': jax.random.normal(ks[5], (E, E), jnp.float32) * 0.02, 'bg': jax.random.normal(ks[6], (E,), jnp.float32) * 0.02, 'wout': jax.random.normal(ks[7], (E, E), jnp.float32) * 0.02, 'aug_balance': jax.random.normal(ks[8], (dk,), jnp.float32) * 0.1}
    _L0_attn_all = _L0_attn_setup()
    _L0_attn_in = {k: v for k, v in _L0_attn_all.items() if k in ('conv_w', 'wq', 'wkg', 'wv', 'wg', 'bg', 'wout', 'aug_balance')}
    del _L0_attn_all

    def _L0_xattn_setup():
        import jax, jax.numpy as jnp
        import numpy as np
        EMBED_DIM = 128
        N_HEAD = 16
        D_K = EMBED_DIM // N_HEAD
        key = jax.random.key(seed)
        kq, kk, kv, kwq, kwk, kwv, kwo = jax.random.split(key, 7)
        B, S, E = (4, 256, EMBED_DIM)
        scale = 1.0 / np.sqrt(E)
        return {'Q': jax.random.normal(kq, (B, S, E), dtype=jnp.float32), 'K': jax.random.normal(kk, (B, S, E), dtype=jnp.float32), 'V': jax.random.normal(kv, (B, S, E), dtype=jnp.float32), 'mask': jnp.zeros((1,), dtype=jnp.bool_), 'Wq': jax.random.normal(kwq, (E, E), dtype=jnp.float32) * scale, 'Wk': jax.random.normal(kwk, (E, E), dtype=jnp.float32) * scale, 'Wv': jax.random.normal(kwv, (E, E), dtype=jnp.float32) * scale, 'Wo': jax.random.normal(kwo, (E, E), dtype=jnp.float32) * scale}
    _L0_xattn_all = _L0_xattn_setup()
    _L0_xattn_in = {k: v for k, v in _L0_xattn_all.items() if k in ('Wq', 'Wk', 'Wv', 'Wo')}
    del _L0_xattn_all

    def _L0_ffn_setup():
        import jax, jax.numpy as jnp
        import numpy as np
        CAPACITY_RATIO = 0.75
        key = jax.random.key(seed)
        k1, k2, k3 = jax.random.split(key, 3)
        B, L, D = (4, 1024, 128)
        x = jax.random.normal(k1, (B, L, D), dtype=jnp.float32)
        w_router = jax.random.normal(k2, (D,), dtype=jnp.float32) * 0.02
        w_block = jax.random.normal(k3, (D, D), dtype=jnp.float32) * 0.02
        return {'x': x, 'w_router': w_router, 'w_block': w_block}
    _L0_ffn_all = _L0_ffn_setup()
    _L0_ffn_in = {k: v for k, v in _L0_ffn_all.items() if k in ('w_router', 'w_block')}
    del _L0_ffn_all
    return {'x': x, 'ctx_1024': ctx_1024, 'mask_1_bf0': mask_1_bf0, 'L0_attn_conv_w': _L0_attn_in['conv_w'], 'L0_attn_wq': _L0_attn_in['wq'], 'L0_attn_wkg': _L0_attn_in['wkg'], 'L0_attn_wv': _L0_attn_in['wv'], 'L0_attn_wg': _L0_attn_in['wg'], 'L0_attn_bg': _L0_attn_in['bg'], 'L0_attn_wout': _L0_attn_in['wout'], 'L0_attn_aug_balance': _L0_attn_in['aug_balance'], 'L0_xattn_Wq': _L0_xattn_in['Wq'], 'L0_xattn_Wk': _L0_xattn_in['Wk'], 'L0_xattn_Wv': _L0_xattn_in['Wv'], 'L0_xattn_Wo': _L0_xattn_in['Wo'], 'L0_ffn_w_router': _L0_ffn_in['w_router'], 'L0_ffn_w_block': _L0_ffn_in['w_block']}

def reference(x, ctx_1024, mask_1_bf0, L0_attn_conv_w, L0_attn_wq, L0_attn_wkg, L0_attn_wv, L0_attn_wg, L0_attn_bg, L0_attn_wout, L0_attn_aug_balance, L0_xattn_Wq, L0_xattn_Wk, L0_xattn_Wv, L0_xattn_Wo, L0_ffn_w_router, L0_ffn_w_block):
    import jax
    import jax.numpy as jnp

    def _L0_attn_ref(x, conv_w, wq, wkg, wv, wg, bg, wout, aug_balance):
        import jax, jax.numpy as jnp
        import numpy as np
        NUM_HEADS = 8
        D_CONV = 4
        NORMALIZER = 16.0
        LN_EPS = 1e-05

        def _causal_dwconv_silu(x, w):
            xt = jnp.transpose(x, (0, 2, 1))
            y = jax.lax.conv_general_dilated(xt, w[:, None, :], window_strides=(1,), padding=[(w.shape[1] - 1, 0)], feature_group_count=x.shape[-1], dimension_numbers=('NCH', 'OIH', 'NCH'))
            return jnp.transpose(jax.nn.silu(y), (0, 2, 1))

        def _gla(q, k, v, gk, scale):
            B, H, L, Dk = q.shape
            Dv = v.shape[-1]

            def step(S, inp):
                qt, kt, vt, gt = inp
                S = S * jnp.exp(gt)[..., None] + kt[..., None] * vt[..., None, :]
                ot = jnp.einsum('bhk,bhkv->bhv', qt * scale, S)
                return (S, ot)
            mv = lambda a: jnp.moveaxis(a, 2, 0)
            S0 = jnp.zeros((B, H, Dk, Dv), q.dtype)
            _, o = jax.lax.scan(step, S0, (mv(q), mv(k), mv(v), mv(gk)))
            return jnp.moveaxis(o, 0, 2)
        B, L, E = x.shape
        H = NUM_HEADS
        xc = _causal_dwconv_silu(x, conv_w)
        q = xc @ wq
        kg = xc @ wkg
        v = xc @ wv
        g = xc @ wg + bg
        gk = jax.nn.log_sigmoid(kg) / NORMALIZER
        k = 1.0 - jnp.exp(gk)
        dkh = q.shape[-1] // H
        to_heads = lambda t: t.reshape(B, L, H, -1).transpose(0, 2, 1, 3)
        qh, kh, vh, gkh = (to_heads(q), to_heads(k), to_heads(v), to_heads(gk))
        scale = dkh ** (-0.5)
        o = _gla(qh, kh, vh, gkh, scale)
        aug = aug_balance.reshape(H, dkh)
        aug_w = jnp.einsum('bhld,hd,bhld->bhl', qh, aug, kh)
        o = o + jax.nn.sigmoid(aug_w[..., None] * vh)
        mu = o.mean(-1, keepdims=True)
        var = o.var(-1, keepdims=True)
        o = (o - mu) * jax.lax.rsqrt(var + LN_EPS)
        o = o.transpose(0, 2, 1, 3).reshape(B, L, E)
        return jax.nn.silu(g) * o @ wout

    def _L0_xattn_ref(Q, K, V, mask, Wq, Wk, Wv, Wo):
        import jax, jax.numpy as jnp
        import numpy as np
        EMBED_DIM = 128
        N_HEAD = 16
        D_K = EMBED_DIM // N_HEAD
        B, S, E = Q.shape
        H, Dk = (N_HEAD, D_K)
        q = (Q @ Wq.T).reshape(B, S, H, Dk).transpose(0, 2, 1, 3)
        k = (K @ Wk.T).reshape(B, S, H, Dk).transpose(0, 2, 1, 3)
        v = (V @ Wv.T).reshape(B, S, H, Dk).transpose(0, 2, 1, 3)
        scores = jnp.einsum('bhqd,bhkd->bhqk', q, k) / jnp.sqrt(jnp.float32(Dk))
        attn = jax.nn.softmax(scores, axis=-1)
        ctx = jnp.einsum('bhqk,bhkd->bhqd', attn, v)
        ctx = ctx.transpose(0, 2, 1, 3).reshape(B, S, E)
        return ctx @ Wo.T

    def _L0_ffn_ref(x, w_router, w_block):
        import jax, jax.numpy as jnp
        import numpy as np
        CAPACITY_RATIO = 0.75
        B, L, D = x.shape
        k = max(1, int(L * CAPACITY_RATIO))
        scores = jnp.einsum('bld,d->bl', x, w_router)
        _, top_idx = jax.lax.top_k(scores, k)
        selected = jnp.take_along_axis(x, top_idx[:, :, None], axis=1)
        processed = jax.nn.gelu(jnp.einsum('bkd,de->bke', selected, w_block))
        batch_idx = jnp.arange(B)[:, None]
        out = x.at[batch_idx, top_idx].set(processed)
        return out
    x = x + _L0_attn_ref(_layernorm(x, axis=-1), L0_attn_conv_w, L0_attn_wq, L0_attn_wkg, L0_attn_wv, L0_attn_wg, L0_attn_bg, L0_attn_wout, L0_attn_aug_balance)
    x = x + _L0_xattn_ref(_layernorm(x, axis=-1), ctx_1024, ctx_1024, mask_1_bf0, L0_xattn_Wq, L0_xattn_Wk, L0_xattn_Wv, L0_xattn_Wo)
    x = x + _L0_ffn_ref(_layernorm(x, axis=-1), L0_ffn_w_router, L0_ffn_w_block)
    return x

_drawn_inputs = setup_inputs


def setup_inputs(seed=0):
    import zlib

    import numpy as np

    out = dict(_drawn_inputs(seed))
    spreads = {}
    factors = {'L0_attn_wkg': 8.0,
     'L0_attn_wv': 3.014,
     'L0_attn_wg': 3.005,
     'L0_attn_bg': 3.731,
     'L0_attn_wout': 3.02,
     'L0_attn_aug_balance': 8.0}
    for name, (base, spread) in spreads.items():
        noise = np.random.default_rng([zlib.crc32(name.encode()), seed]).standard_normal(out[name].shape)
        drawn = base * np.exp(spread * noise) if base else spread * noise
        out[name] = jnp.asarray(drawn.astype(out[name].dtype))
    for name, factor in factors.items():
        out[name] = (out[name] * factor).astype(out[name].dtype)
    return out
```

```python
import concourse.bass as bass
from concourse import mybir
from contextlib import ExitStack


def decoder_layer(
    nc: bass.Bass,
    x: bass.AP, ctx_in: bass.AP, conv_w: bass.AP, wq: bass.AP, wkg: bass.AP, wv: bass.AP, wg: bass.AP,
    bg: bass.AP, wout: bass.AP, aug: bass.AP, WqT: bass.AP, WkT: bass.AP, WvT: bass.AP, WoT: bass.AP,
    w_router: bass.AP, w_block: bass.AP, out: bass.AP,
):
    fp32 = mybir.dt.float32
    bf16 = mybir.dt.bfloat16
    u32 = mybir.dt.uint32
    ALU = mybir.AluOpType
    ACT = mybir.ActivationFunctionType
    AX = mybir.AxisListType

    B, L, E = x.shape
    P = 128
    TPG = 4
    NT = B * L // P
    NG = NT // TPG
    GT = TPG * P
    SEQ = GT // L
    DK = wq.shape[1]
    H = 8
    DKH, DVH = DK // H, E // H
    XH = 16
    XD = E // XH
    NB = 2 * H
    KH = TPG * L
    TAPS = conv_w.shape[1]
    PADL = TAPS - 1 + L
    CH = 8
    NCH = L // CH
    REF = CH // 2 - 1
    NORMALIZER = 16.0
    LEAST_LOG = -20.0 * NORMALIZER
    EPS = 1e-5
    KEEP = max(1, int(L * 0.75))
    GELU_C, GELU_A = 0.7978845608028654, 0.044715
    PAIRS = XH // 2
    VC = XD + 1

    x_tiles = x.rearrange("b l e -> (b l) e").rearrange("(t p) e -> p t e", p=P)
    ctx_tiles = ctx_in.rearrange("b l e -> (b l) e").rearrange("(t p) e -> p t e", p=P)
    out_tiles = out.rearrange("b l e -> (b l) e").rearrange("(t p) e -> p t e", p=P)

    stack = ExitStack()
    with stack:
        def sb(name, cols, dt=fp32, parts=P):
            return stack.enter_context(nc.sbuf_tensor(name, [parts, cols], dt))

        def sem(name):
            return stack.enter_context(nc.semaphore(name))

        def cut(t, *dims):
            a = t[:, :]
            names = "abcd"[:len(dims)]
            return a.rearrange(f"p ({' '.join(names)}) -> p {' '.join(names)}",
                               **{n: d for n, d in zip(names, dims)})

        ident = sb("ident", P)
        ident_b = sb("ident_b", P, bf16)
        causal = sb("causal", L, u32)
        causal_f = sb("causal_f", L)
        before = sb("before", L)
        same = sb("same", L)
        block_of = sb("block_of", NB)
        aug_sel = sb("aug_sel", NB)
        carry = sb("carry", KH)
        minus_half = sb("minus_half", TPG * H)
        eps_s = sb("eps_s", TPG)
        bearer = sb("bearer", 7)
        wq_s, wkg_s = sb("wq_s", DK), sb("wkg_s", DK)
        wv_s, wg_s, wout_s = sb("wv_s", E), sb("wg_s", E), sb("wout_s", E)
        WqT_s, WkT_s, WvT_s, WoT_s = sb("WqT_s", E), sb("WkT_s", E), sb("WvT_s", E), sb("WoT_s", E)
        wblk_s = sb("wblk_s", E)
        wr_s = sb("wr_s", 1)
        wr_rep = sb("wr_rep", L)
        conv_s, bg_s, aug_s = sb("conv_s", TAPS), sb("bg_s", 1), sb("aug_s", 1)
        conv_half, bg_half = sb("conv_half", TAPS), sb("bg_half", 1)

        x_all = sb("x_all", NT * E)
        xa = cut(x_all, NT, E)
        st1, mv1, ve1, rs1 = sb("st1", TPG * 6), sb("mv1", TPG * 2), sb("ve1", TPG), sb("rs1", TPG)
        xn1 = sb("xn1", GT)
        xpad = sb("xpad", SEQ * PADL)
        xpad_v = cut(xpad, SEQ, PADL)
        y = sb("y", GT)
        th1 = sb("th1", GT)
        xcT = sb("xcT", GT)
        qk = sb("qk", 2 * KH)
        q_s, kg_s = qk[:, 0:KH], qk[:, KH:2 * KH]
        ab, ex, ln1p, lsig = sb("ab", KH), sb("ex", KH), sb("ln1p", KH), sb("lsig", KH)
        decay, key, lclip, G = sb("decay", KH), sb("key", KH), sb("lclip", KH), sb("G", KH)
        dq, dr = sb("dq", KH), sb("dr", TPG * NCH * NCH)
        drc = sb("drc", TPG * NCH * NCH)
        e_q, e_k, e_r = sb("e_q", KH), sb("e_k", KH), sb("e_r", TPG * NCH * NCH)
        qs, ke, qkp = sb("qs", KH), sb("ke", KH), sb("qkp", KH)
        kc = sb("kc", TPG * NCH * L)
        kc_m = cut(kc, TPG, NCH, L)
        q_bd = sb("q_bd", NB * KH)
        q_bdv = cut(q_bd, NB, KH)
        vt = sb("vt", GT)
        v_bd = sb("v_bd", 2 * 2 * 2 * E)
        v_bdv = v_bd[:, :].rearrange("p (j x w f) -> p j x w f", j=2, x=2, w=2)
        at = sb("at", 2 * NB * L)
        at_m = cut(at, 2, NB, L)
        at_c = at[:, :].rearrange("p (j n c s) -> p j c n s", j=2, n=NB, c=NCH)
        gh, tg, sg = sb("gh", GT), sb("tg", GT), sb("sg", GT)
        z, tz, o_s, dev, sq1, on = (sb(n, GT) for n in ("z", "tz", "o_s", "dev", "sq1", "on"))
        osum, omean, oss, ove, ors = (sb(n, TPG * H) for n in ("osum", "omean", "oss", "ove", "ors"))
        ogT = sb("ogT", GT)
        c_s, cT = sb("c_s", GT), sb("cT", GT)
        kx = sb("kx", GT)
        k_bd = sb("k_bd", XH * GT)
        k_bdv = cut(k_bd, XH, GT)
        v_x = sb("v_x", SEQ * PAIRS * 2 * VC)
        v_xv = cut(v_x, SEQ, PAIRS, 2 * VC)
        x1 = sb("x1", GT)

        st2, mv2, ve2, rs2 = sb("st2", TPG * 6), sb("mv2", TPG * 2), sb("ve2", TPG), sb("rs2", TPG)
        xn2, xT2, qT = sb("xn2", GT), sb("xT2", GT), sb("qT", GT)
        nmax = sb("nmax", XH, bf16)
        pr = sb("pr", 2 * XH * L)
        pr_v = cut(pr, 2, XH * L)
        prT = sb("prT", PAIRS * P)
        prT_v = cut(prT, PAIRS, P)
        rden = sb("rden", XH)
        cx, cxT, x2 = sb("cx", GT), sb("cxT", GT), sb("x2", GT)
        st3, mv3, ve3, rs3 = sb("st3", TPG * 6), sb("mv3", TPG * 2), sb("ve3", TPG), sb("rs3", TPG)
        xn3, xT3 = sb("xn3", GT), sb("xT3", GT)
        yh, ysq, yu, yv, yt, gl = (sb(n, GT) for n in ("yh", "ysq", "yu", "yv", "yt", "gl"))
        rs_all = sb("rs_all", KH)
        own, r_own = sb("own", KH), sb("r_own", TPG)
        above, tied, tiedb, cnt = sb("above", KH), sb("tied", KH), sb("tiedb", KH), sb("cnt", KH)
        rank, taken = sb("rank", TPG), sb("taken", TPG)
        yout = sb("yout", GT)

        def ps(name, cols):
            return stack.enter_context(nc.psum_tensor(name, [P, cols], fp32))

        PA0, PA1, AT = ps("PA0", 512), ps("PA1", 512), ps("AT", 1024)
        S, PT, PB = ps("S", 1024), ps("PT", 512), ps("PB", 512)
        AT0, AT1 = AT[:, 0:512], AT[:, 512:1024]

        w_in, x_in, x_rest, c_in = sem("w_in"), sem("x_in"), sem("x_rest"), sem("c_in")
        consts, consts2, derived = sem("consts"), sem("consts2"), sem("derived")
        q_clear, clear = sem("q_clear"), sem("clear")
        s_st1, s_mv1, s_ve1, s_rs1, s_xn1 = (sem(n) for n in ("s_st1", "s_mv1", "s_ve1", "s_rs1", "s_xn1"))
        s_xT, s_xpad, s_conv, s_th1, s_xc = (sem(n) for n in ("s_xT", "s_xpad", "s_conv", "s_th1", "s_xc"))
        s_QK, s_V, s_Gt, s_qk, s_vt = (sem(n) for n in ("s_QK", "s_V", "s_Gt", "s_qk", "s_vt"))
        s_ab, s_ex, s_ln, s_lsig, s_decay, s_key = (
            sem(n) for n in ("s_ab", "s_ex", "s_ln", "s_lsig", "s_decay", "s_key"))
        s_lclip, s_G, s_dq, s_dr, s_drc = (sem(n) for n in ("s_lclip", "s_G", "s_dq", "s_dr", "s_drc"))
        s_eq, s_ek, s_er, s_qs, s_ke, s_qkp, s_kc = (
            sem(n) for n in ("s_eq", "s_ek", "s_er", "s_qs", "s_ke", "s_qkp", "s_kc"))
        s_qbd, s_vbd = sem("s_qbd"), sem("s_vbd")
        s_AUG, s_AT, s_at, s_AV = (sem(n) for n in ("s_AUG", "s_AT", "s_at", "s_AV"))
        s_gh, s_tg, s_sg = (sem(n) for n in ("s_gh", "s_tg", "s_sg"))
        s_z, s_tz, s_o, s_osum, s_omean, s_dev, s_sq1, s_oss = (
            sem(n) for n in ("s_z", "s_tz", "s_o", "s_osum", "s_omean", "s_dev", "s_sq1", "s_oss"))
        s_ove, s_ors, s_on, s_OT, s_og, s_Y, s_x1 = (
            sem(n) for n in ("s_ove", "s_ors", "s_on", "s_OT", "s_og", "s_Y", "s_x1"))
        s_CT, s_cT, s_KX, s_kx, s_VX, s_vx = (sem(n) for n in ("s_CT", "s_cT", "s_KX", "s_kx", "s_VX", "s_vx"))
        s_kbd = sem("s_kbd")
        s_st2, s_mv2, s_ve2, s_rs2, s_xd2, s_xn2 = (
            sem(n) for n in ("s_st2", "s_mv2", "s_ve2", "s_rs2", "s_xd2", "s_xn2"))
        s_T2, s_xT2, s_Q, s_qT = (sem(n) for n in ("s_T2", "s_xT2", "s_Q", "s_qT"))
        s_S, s_max, s_fold, s_exp = (sem(n) for n in ("s_S", "s_max", "s_fold", "s_exp"))
        s_PT, s_prT = sem("s_PT"), sem("s_prT")
        s_PV, s_rden, s_cx = (sem(n) for n in ("s_PV", "s_rden", "s_cx"))
        s_CX, s_cxT, s_WO, s_x2 = (sem(n) for n in ("s_CX", "s_cxT", "s_WO", "s_x2"))
        s_st3, s_mv3, s_ve3, s_rs3, s_xd3, s_xn3 = (
            sem(n) for n in ("s_st3", "s_mv3", "s_ve3", "s_rs3", "s_xd3", "s_xn3"))
        s_T3, s_xT3, s_FF, s_RT = (sem(n) for n in ("s_T3", "s_xT3", "s_FF", "s_RT"))
        s_yh, s_ysq, s_yu, s_yv, s_yt, s_gl = (sem(n) for n in ("s_yh", "s_ysq", "s_yu", "s_yv", "s_yt", "s_gl"))
        s_rall, s_own, s_rown, s_above, s_tied, s_tiedb, s_cnt, s_rank, s_taken = (
            sem(n) for n in ("s_rall", "s_own", "s_rown", "s_above", "s_tied", "s_tiedb", "s_cnt", "s_rank",
                             "s_taken"))
        s_sel, s_yout, s_out = sem("s_sel"), sem("s_yout"), sem("s_out")

        WEIGHTS = [(wq_s, wq), (wkg_s, wkg), (wv_s, wv), (wg_s, wg), (wout_s, wout), (WqT_s, WqT),
                   (WkT_s, WkT), (WvT_s, WvT), (WoT_s, WoT), (wblk_s, w_block), (conv_s, conv_w),
                   (wr_s, w_router), (bg_s, bg), (aug_s, None)]
        W_IN = 16 * (len(WEIGHTS) + 1)

        def bear(n):
            nc.vector.tensor_copy(bearer[:, 1 + n:2 + n], bearer[:, 0:1])

        block = stack.enter_context(nc.Block())

        @block.sync
        def _(sp):
            def tiles_of(view, g):
                return view[:, bass.ds(TPG * g, TPG), :]

            def load_ctx(g):
                sp.wait_ge(s_CT, g)
                sp.dma_start(cut(c_s, TPG, E), tiles_of(ctx_tiles, g)).then_inc(c_in, 16)

            def queries_to_blocks(g):
                sp.wait_ge(s_qs, g + 1)
                sp.wait_ge(s_AT, 2 * g)
                for n in range(NB):
                    sp.dma_start(q_bdv[8 * n:8 * n + 8, n, :], qs[8 * n:8 * n + 8, :]).then_inc(s_qbd, 16)

            def values_to_blocks(g):
                sp.wait_ge(s_vt, g + 1)
                sp.wait_ge(s_AV, 2 * g)
                for half in range(2):
                    for w in range(2):
                        src = vt[L * half:L * half + L, :].rearrange("p (j w f) -> p j w f", j=2, w=2)[:, :, w, :]
                        sp.dma_start(v_bdv[L * w:L * w + L, :, half, w, :], src).then_inc(s_vbd, 16)

            def keys_to_blocks(g):
                sp.wait_ge(s_S, TPG * g)
                sp.wait_ge(s_kx, g + 1)
                for h in range(XH):
                    sp.dma_start(k_bdv[8 * h:8 * h + 8, h, :], kx[8 * h:8 * h + 8, :]).then_inc(s_kbd, 16)

            def store(g):
                sp.wait_ge(s_yout, g + 1)
                sp.dma_start(tiles_of(out_tiles, g), cut(yout, TPG, E)).then_inc(s_out, 16)

            sp.dma_start(xa[:, 0:TPG, :], x_tiles[:, 0:TPG, :]).then_inc(x_in, 16)
            load_ctx(0)
            for dst, src in WEIGHTS[:-1]:
                sp.dma_start(dst[:, :], src).then_inc(w_in, 16)
            for half in range(2):
                sp.dma_start(aug_s[DK * half:DK * half + DK, :], aug).then_inc(w_in, 16)
            sp.dma_start(xa[:, TPG:NT, :], x_tiles[:, TPG:NT, :]).then_inc(x_rest, 16)
            sp.wait_ge(clear, 3)
            sp.wait_ge(q_clear, 1)
            load_ctx(1)
            values_to_blocks(0)
            queries_to_blocks(0)
            keys_to_blocks(0)

            def body(g):
                load_ctx(g + 2)
                values_to_blocks(g + 1)
                queries_to_blocks(g + 1)
                keys_to_blocks(g + 1)
                store(g)

            body(0)
            with sp.Fori(1, NG - 2) as g:
                body(g)
            values_to_blocks(NG - 1)
            queries_to_blocks(NG - 1)
            keys_to_blocks(NG - 1)
            store(NG - 2)
            store(NG - 1)
            sp.wait_ge(s_out, 16 * NG)

        @block.gpsimd
        def _(pool):
            nc.gpsimd.memset(ident[:, :], 0.0).then_inc(consts, 1)
            nc.gpsimd.memset(causal_f[:, :], 1.0).then_inc(consts, 1)
            nc.gpsimd.memset(before[:, :], 1.0).then_inc(consts, 1)
            nc.gpsimd.memset(same[:, :], 0.0).then_inc(consts, 1)
            nc.gpsimd.memset(block_of[:, :], 1.0).then_inc(consts, 1)
            nc.gpsimd.memset(carry[:, :], 1.0).then_inc(consts, 1)
            nc.gpsimd.memset(minus_half[:, :], -0.5).then_inc(consts, 1)
            nc.gpsimd.memset(xpad[:, :], 0.0).then_inc(consts, 1)
            nc.gpsimd.memset(eps_s[:, :], EPS).then_inc(consts, 1)
            pool.wait_ge(consts, 9)
            made = 0

            def select(t, keep, fill, base, step, by_row):
                nonlocal made
                nc.gpsimd.affine_select(out=t, in_=t, compare_op=keep, fill=fill, base=base,
                                        pattern=[[step, t.shape[1]]], channel_multiplier=by_row).then_inc(consts2, 1)
                made += 1
                pool.wait_ge(consts2, made)

            select(ident[:, :], ALU.not_equal, 1.0, 0, -1, 1)
            for half in range(2):
                rows = slice(L * half, L * half + L)
                select(causal_f[rows, :], ALU.is_ge, 0.0, 0, 1, -1)
                select(before[rows, :], ALU.is_gt, 0.0, 0, -1, 1)
                select(same[rows, :], ALU.not_equal, 1.0, 0, -1, 1)
            select(block_of[:, :], ALU.is_ge, 0.0, 0, -8, 1)
            select(block_of[:, :], ALU.is_ge, 0.0, 7, 8, -1)
            nc.gpsimd.memset(cut(carry, TPG, L)[:, :, 0:1], 0.0).then_inc(consts2, 1)

            def scales(g, s_mv, s_ve, s_rs, s_xn, mv, ve, rs):
                pool.wait_ge(s_mv, g + 1)
                nc.gpsimd.tensor_tensor(cut(ve, TPG, 1), cut(mv, TPG, 2)[:, :, 1:2], cut(eps_s, TPG, 1),
                                        ALU.add).then_inc(s_ve, 1)
                pool.wait_ge(s_ve, g + 1)
                pool.wait_ge(s_xn, g)
                nc.gpsimd.tensor_tensor(rs[:, :], ve[:, :], minus_half[:, 0:TPG], ALU.pow).then_inc(s_rs, 1)

            def norm(g, s_mv, s_ve, s_rs, s_xd, s_xn, s_read, src, mv, ve, rs, dst):
                scales(g, s_mv, s_ve, s_rs, s_xn, mv, ve, rs)
                for s in s_read:
                    pool.wait_ge(s, g)
                nc.gpsimd.tensor_tensor(cut(dst, TPG, E), cut(src, TPG, E),
                                        cut(mv, TPG, 2)[:, :, 0:1].to_broadcast([P, TPG, E]),
                                        ALU.subtract).then_inc(s_xd, 1)
                pool.wait_ge(s_xd, g + 1)
                pool.wait_ge(s_rs, g + 1)
                nc.gpsimd.tensor_tensor(cut(dst, TPG, E), cut(dst, TPG, E),
                                        rs[:, :].unsqueeze(2).to_broadcast([P, TPG, E]),
                                        ALU.mult).then_inc(s_xn, 1)

            def norm_a(g):
                scales(g, s_mv1, s_ve1, s_rs1, s_xn1, mv1, ve1, rs1)

            def norm_b2(g):
                norm(g, s_mv2, s_ve2, s_rs2, s_xd2, s_xn2, [s_T2], x1, mv2, ve2, rs2, xn2)

            def norm_b3(g):
                norm(g, s_mv3, s_ve3, s_rs3, s_xd3, s_xn3, [s_T3, s_yout], x2, mv3, ve3, rs3, xn3)

            def keys(g):
                pool.wait_ge(s_ke, g + 1)
                pool.wait_ge(s_er, g + 1)
                pool.wait_ge(s_AT, 2 * g)
                kev = cut(ke, TPG, NCH, CH)
                erv = cut(e_r, TPG, NCH, NCH)
                for i in range(TPG):
                    nc.gpsimd.tensor_tensor(
                        kc[:, i * NCH * L:(i + 1) * NCH * L].rearrange(
                            "p (c d s) -> p c d s", c=NCH, d=NCH),
                        kev[:, i, :, :].unsqueeze(1).to_broadcast([P, NCH, NCH, CH]),
                        erv[:, i, :, :].unsqueeze(3).to_broadcast([P, NCH, NCH, CH]), ALU.mult).then_inc(s_kc, 1)

            def group_norm(g):
                pool.wait_ge(s_ove, g + 1)
                nc.gpsimd.tensor_tensor(ors[:, :], ove[:, :], minus_half[:, :], ALU.pow).then_inc(s_ors, 1)
                pool.wait_ge(s_ors, g + 1)
                pool.wait_ge(s_OT, g)
                nc.gpsimd.tensor_tensor(cut(on, TPG * H, DVH), cut(dev, TPG * H, DVH),
                                        ors[:, :].unsqueeze(2).to_broadcast([P, TPG * H, DVH]),
                                        ALU.mult).then_inc(s_on, 1)

            norm_a(0)
            nc.gpsimd.memset(q_bd[:, :], 0.0).then_inc(q_clear, 1)
            keys(0)
            norm_a(1)
            group_norm(0)

            def body(g):
                norm_b2(g)
                keys(g + 1)
                norm_a(g + 2)
                group_norm(g + 1)
                norm_b3(g)

            body(0)
            with pool.Fori(1, NG - 2) as g:
                body(g)
            norm_b2(NG - 2)
            keys(NG - 1)
            group_norm(NG - 1)
            norm_b3(NG - 2)
            norm_b2(NG - 1)
            norm_b3(NG - 1)

        @block.tensor
        def _(pe):
            def to_features(dst, src):
                for i in range(TPG):
                    last = nc.tensor.transpose(dst[:, P * i:P * i + P], src[:, P * i:P * i + P], ident[:, :])
                return last

            def transpose_x(g):
                pe.wait_ge(s_xn1, g + 1)
                pe.wait_ge(s_og, g)
                to_features(PA0, xn1).then_inc(s_xT, 1)

            def transpose_ctx(g):
                pe.wait_ge(c_in, 16 * (g + 1))
                pe.wait_ge(s_x1, g)
                to_features(PA1, c_s).then_inc(s_CT, 1)

            def context_keys(g):
                pe.wait_ge(s_cT, g + 1)
                pe.wait_ge(s_at, 2 * g)
                nc.tensor.matmul(AT1, WkT_s[:, :], cT[:, :], start=True, stop=True).then_inc(s_KX, 1)

            def context_values(g):
                pe.wait_ge(s_cT, g + 1)
                pe.wait_ge(s_exp, TPG * g)
                for b in range(SEQ):
                    for half in range(2):
                        last = nc.tensor.matmul(S[L * half:L * half + L, E * b:E * b + E], cT[:, L * b:L * b + L],
                                                WvT_s[:, :], start=True, stop=True)
                last.then_inc(s_VX, 1)

            def project(g):
                xc_h = xcT[:, :].rearrange("p (i x t) -> p i x t", i=TPG, x=2)
                pe.wait_ge(s_xc, g + 1)
                pe.wait_ge(s_xpad, g + 1)
                for n, w in enumerate((wq_s, wkg_s)):
                    for half in range(2):
                        last = nc.tensor.matmul(PA0[L * half:L * half + L, KH * n:KH * n + KH], w[:, :],
                                                xc_h[:, :, half, :], start=True, stop=True)
                last.then_inc(s_QK, 1)
                pe.wait_ge(s_cT, g + 1)
                for i in range(TPG):
                    last = nc.tensor.matmul(PA1[:, E * i:E * i + E], xcT[:, P * i:P * i + P], wv_s[:, :],
                                            start=True, stop=True)
                last.then_inc(s_V, 1)
                pe.wait_ge(s_at, 2 * g)
                nc.tensor.matmul(AT0, wg_s[:, :], xcT[:, :], start=True, stop=True).then_inc(s_Gt, 1)

            def aug_weights(g):
                pe.wait_ge(s_qkp, g + 1)
                pe.wait_ge(s_qk, g + 1)
                for i in range(TPG):
                    for half in range(2):
                        last = nc.tensor.matmul(PA0[L * half:L * half + L, H * i:H * i + H],
                                                qkp[:, L * i:L * i + L], aug_sel[:, H * half:H * half + H],
                                                start=True, stop=True)
                last.then_inc(s_AUG, 1)

            def scores(g, j):
                pe.wait_ge(s_kc, TPG * g + 2 * j + 2)
                if j == 0:
                    pe.wait_ge(s_qbd, 16 * NB * (g + 1))
                    pe.wait_ge(s_gh, g + 1)
                    pe.wait_ge(s_kx, g + 1)
                else:
                    pe.wait_ge(s_at, 2 * g + j)
                for c in range(NCH):
                    for w in range(2):
                        i = 2 * j + w
                        last = nc.tensor.matmul(AT[L * w:L * w + L, c * NB * CH:(c + 1) * NB * CH],
                                                kc_m[:, i, c, :],
                                                q_bdv[:, :, L * i + CH * c:L * i + CH * c + CH],
                                                start=True, stop=True)
                last.then_inc(s_AT, 1)

            def attend(g, j):
                pe.wait_ge(s_at, 2 * g + j + 1)
                if j == 0:
                    pe.wait_ge(s_vbd, 64 * (g + 1))
                    pe.wait_ge(s_vt, g + 1)
                o_v = PA1[:, :].rearrange("p (j w f) -> p j w f", j=2, w=2)
                for h in range(H):
                    for half in range(2):
                        n = H * half + h
                        last = nc.tensor.matmul(o_v[L * half:L * half + L, j, :, DVH * h:DVH * h + DVH],
                                                at_m[:, j, n, :], v_bdv[:, j, half, :, DVH * h:DVH * h + DVH],
                                                start=True, stop=True)
                last.then_inc(s_AV, 1)

            def transpose_o(g):
                pe.wait_ge(s_on, g + 1)
                pe.wait_ge(s_z, g + 1)
                to_features(PA0, on).then_inc(s_OT, 1)

            def gla_out(g):
                pe.wait_ge(s_og, g + 1)
                pe.wait_ge(s_o, g + 1)
                for i in range(TPG):
                    last = nc.tensor.matmul(PA1[:, E * i:E * i + E], ogT[:, P * i:P * i + P], wout_s[:, :],
                                            start=True, stop=True)
                last.then_inc(s_Y, 1)

            def queries(g):
                pe.wait_ge(s_xn2, g + 1)
                pe.wait_ge(s_rall, g)
                to_features(PT, xn2).then_inc(s_T2, 1)
                pe.wait_ge(s_xT2, g + 1)
                pe.wait_ge(s_yh, g)
                nc.tensor.matmul(PB[:, :], WqT_s[:, :], xT2[:, :], start=True, stop=True).then_inc(s_Q, 1)

            def x_scores(g, i):
                if i == 0:
                    pe.wait_ge(s_qT, g + 1)
                    pe.wait_ge(s_kbd, 16 * XH * (g + 1))
                    pe.wait_ge(s_vx, g + 1)
                else:
                    pe.wait_ge(s_exp, TPG * g + i)
                hh = XH // 2
                for n in range(2):
                    for half in range(2):
                        b = 2 * i + half
                        last = nc.tensor.matmul(S[L * half:L * half + L, 512 * n:512 * n + 512],
                                                qT[:, L * b:L * b + L],
                                                k_bdv[:, hh * n:hh * n + hh, L * b:L * b + L], start=True, stop=False,
                                                skip_group_check=True)
                last.then_inc(s_S, 1)

            def less_max(g, i):
                pe.wait_ge(s_max, TPG * g + i + 1)
                hh = XH // 2
                for n in range(2):
                    last = nc.tensor.matmul(S[:, 512 * n:512 * n + 512], ident_b[:, :],
                                            nmax[:, hh * n:hh * n + hh].unsqueeze(2).to_broadcast([P, hh, L]),
                                            start=False, stop=True, skip_group_check=True)
                last.then_inc(s_fold, 1)

            def x_attend(g, i, n):
                hp = PAIRS // 2
                if n == 0:
                    pe.wait_ge(s_exp, TPG * g + i + 1)
                pe.wait_ge(s_prT, 2 * (TPG * g + i) + n)
                if i == 0 and n == 0:
                    pe.wait_ge(s_xT2, g + 1)
                for p in range(hp):
                    last = nc.tensor.transpose(PT[:, P * p:P * p + P],
                                               pr_v[:, i % 2, P * (hp * n + p):P * (hp * n + p) + P], ident[:, :])
                last.then_inc(s_PT, 1)

            def x_values(g, i, n):
                hp = PAIRS // 2
                pe.wait_ge(s_prT, 2 * (TPG * g + i) + n + 1)
                if n == 0:
                    pe.wait_ge(s_cx, TPG * g + i)
                    if i == 0:
                        pe.wait_ge(s_qT, g + 1)
                for p in range(hp * n, hp * n + hp):
                    for half in range(2):
                        last = nc.tensor.matmul(PB[L * half:L * half + L, 2 * VC * p:2 * VC * p + 2 * VC],
                                                prT_v[:, p, L * half:L * half + L], v_xv[:, 2 * i + half, p, :],
                                                start=True, stop=True)
                if n == 1:
                    last.then_inc(s_PV, 1)

            def x_out(g):
                pe.wait_ge(s_cx, TPG * g + TPG)
                pe.wait_ge(s_prT, 2 * TPG * (g + 1))
                to_features(PT, cx).then_inc(s_CX, 1)

            def x_out2(g):
                pe.wait_ge(s_cxT, g + 1)
                for i in range(TPG):
                    last = nc.tensor.matmul(PB[:, E * i:E * i + E], cxT[:, P * i:P * i + P], WoT_s[:, :],
                                            start=True, stop=True)
                last.then_inc(s_WO, 1)

            def ffn(g):
                pe.wait_ge(s_xn3, g + 1)
                pe.wait_ge(s_cxT, g + 1)
                to_features(PT, xn3).then_inc(s_T3, 1)
                pe.wait_ge(s_xT3, g + 1)
                x_h = xT3[:, :].rearrange("p (i x t) -> p i x t", i=TPG, x=2)
                for half in range(2):
                    last = nc.tensor.matmul(PT[L * half:L * half + L, 0:KH], wr_rep[:, :], x_h[:, :, half, :],
                                            start=True, stop=True)
                last.then_inc(s_RT, 1)
                pe.wait_ge(s_x2, g + 1)
                for i in range(TPG):
                    last = nc.tensor.matmul(PB[:, E * i:E * i + E], xT3[:, P * i:P * i + P], wblk_s[:, :],
                                            start=True, stop=True)
                last.then_inc(s_FF, 1)

            pe.wait_ge(w_in, W_IN)
            pe.wait_ge(consts2, 10)
            pe.wait_ge(derived, 1)
            transpose_x(0)
            transpose_ctx(0)
            context_keys(0)
            project(0)
            aug_weights(0)
            scores(0, 0)
            scores(0, 1)
            attend(0, 0)
            attend(0, 1)
            context_values(0)
            transpose_o(0)
            gla_out(0)

            def body(g, more):
                if more:
                    transpose_x(g + 1)
                    transpose_ctx(g + 1)
                queries(g)
                x_scores(g, 0)
                if more:
                    context_keys(g + 1)
                less_max(g, 0)
                if more:
                    project(g + 1)
                x_scores(g, 1)
                x_attend(g, 0, 0)
                x_values(g, 0, 0)
                less_max(g, 1)
                x_attend(g, 0, 1)
                x_values(g, 0, 1)
                if more:
                    aug_weights(g + 1)
                x_scores(g, 2)
                x_attend(g, 1, 0)
                x_values(g, 1, 0)
                less_max(g, 2)
                x_attend(g, 1, 1)
                x_values(g, 1, 1)
                if more:
                    scores(g + 1, 0)
                x_scores(g, 3)
                x_attend(g, 2, 0)
                x_values(g, 2, 0)
                less_max(g, 3)
                x_attend(g, 2, 1)
                x_values(g, 2, 1)
                if more:
                    scores(g + 1, 1)
                x_attend(g, 3, 0)
                if more:
                    attend(g + 1, 0)
                x_values(g, 3, 0)
                x_attend(g, 3, 1)
                x_values(g, 3, 1)
                if more:
                    attend(g + 1, 1)
                x_out(g)
                if more:
                    context_values(g + 1)
                x_out2(g)
                if more:
                    transpose_o(g + 1)
                ffn(g)
                if more:
                    gla_out(g + 1)

            body(0, True)
            with pe.Fori(1, NG - 2) as g:
                body(g, True)
            body(NG - 2, True)
            body(NG - 1, False)

        @block.scalar
        def _(act):
            def a_features(g):
                act.wait_ge(s_xT, g + 1)
                act.wait_ge(s_conv, TAPS * g)
                nc.scalar.copy(xpad_v[:, :, TAPS - 1:PADL], cut(PA0, SEQ, L)).then_inc(s_xpad, 1)
                act.wait_ge(s_CT, g + 1)
                act.wait_ge(s_VX, g)
                nc.scalar.copy(cT[:, :], PA1[:, :]).then_inc(s_cT, 1)

            def a_silu(g):
                act.wait_ge(s_conv, TAPS * (g + 1))
                nc.scalar.activation(th1[:, :], y[:, :], ACT.Tanh).then_inc(s_th1, 1)

            def a_keys(g):
                act.wait_ge(s_KX, g + 1)
                act.wait_ge(s_kbd, 16 * XH * g)
                nc.scalar.copy(kx[:, :], AT1).then_inc(s_kx, 1)

            def a_proj(g):
                act.wait_ge(s_QK, g + 1)
                act.wait_ge(s_qkp, g)
                nc.scalar.copy(qk[:, :], PA0[:, :]).then_inc(s_qk, 1)
                act.wait_ge(s_Gt, g + 1)
                act.wait_ge(s_sg, g)
                nc.scalar.activation(gh[:, :], AT0, ACT.Identity, bias=bg_half[:, :], scale=0.5).then_inc(s_gh, 1)
                act.wait_ge(s_V, g + 1)
                act.wait_ge(s_vbd, 64 * g)
                act.wait_ge(s_z, g)
                nc.scalar.copy(vt[:, :], PA1[:, :]).then_inc(s_vt, 1)
                act.wait_ge(s_gh, g + 1)
                nc.scalar.activation(tg[:, :], gh[:, :], ACT.Tanh).then_inc(s_tg, 1)

            def a_log(g):
                act.wait_ge(s_qk, g + 1)
                nc.scalar.activation(ab[:, :], kg_s, ACT.Abs).then_inc(s_ab, 1)
                act.wait_ge(s_ab, g + 1)
                nc.scalar.activation(ex[:, :], ab[:, :], ACT.Exp, scale=-1.0).then_inc(s_ex, 1)
                act.wait_ge(s_ex, g + 1)
                act.wait_ge(s_lsig, g)
                nc.scalar.activation(ln1p[:, :], ex[:, :], ACT.Ln, bias=1.0).then_inc(s_ln, 1)

            def a_decays(g):
                act.wait_ge(s_lsig, g + 1)
                nc.scalar.activation(decay[:, :], lsig[:, :], ACT.Exp, scale=1.0 / NORMALIZER).then_inc(s_decay, 1)
                act.wait_ge(s_dq, g + 1)
                nc.scalar.activation(e_q[:, :], dq[:, :], ACT.Exp, scale=1.0 / NORMALIZER).then_inc(s_eq, 1)
                nc.scalar.activation(e_k[:, :], dq[:, :], ACT.Exp, scale=-1.0 / NORMALIZER).then_inc(s_ek, 1)
                act.wait_ge(s_drc, g + 1)
                act.wait_ge(s_kc, TPG * g)
                nc.scalar.activation(e_r[:, :], drc[:, :], ACT.Exp, scale=1.0 / NORMALIZER).then_inc(s_er, 1)

            def a_aug(g):
                act.wait_ge(s_z, g + 1)
                act.wait_ge(s_o, g)
                nc.scalar.activation(tz[:, :], z[:, :], ACT.Tanh, scale=0.5).then_inc(s_tz, 1)

            def a_square(g):
                act.wait_ge(s_dev, g + 1)
                act.wait_ge(s_oss, g)
                nc.scalar.activation(sq1[:, :], dev[:, :], ACT.Square).then_inc(s_sq1, 1)

            def a_values(g):
                act.wait_ge(s_VX, g + 1)
                act.wait_ge(s_PV, TPG * g)
                for half in range(2):
                    rows = slice(L * half, L * half + L)
                    dst = v_x[rows, :].rearrange("p (b q u v) -> p b q u v", b=SEQ, q=PAIRS, u=2)[:, :, :, half, 0:XD]
                    src = S[rows, :].rearrange("p (b q u v) -> p b q u v", b=SEQ, q=PAIRS, u=2)[:, :, :, half, :]
                    last = nc.scalar.copy(dst, src)
                last.then_inc(s_vx, 1)

            def b_queries(g):
                act.wait_ge(s_T2, g + 1)
                nc.scalar.copy(xT2[:, :], PT[:, :]).then_inc(s_xT2, 1)
                act.wait_ge(s_Q, g + 1)
                act.wait_ge(s_S, TPG * g)
                nc.scalar.activation(qT[:, :], PB[:, :], ACT.Copy, scale=float(XD) ** -0.5).then_inc(s_qT, 1)

            def b_exp(g, i):
                act.wait_ge(s_fold, TPG * g + i + 1)
                nc.scalar.activation(pr_v[:, i % 2, :], S[:, :], ACT.Exp).then_inc(s_exp, 1)

            def b_probs(g, i):
                act.wait_ge(s_PT, 2 * (TPG * g + i) + 2)
                nc.scalar.copy(prT[:, 512:1024], PT[:, :]).then_inc(s_prT, 1)

            def b_out(g):
                act.wait_ge(s_CX, g + 1)
                nc.scalar.copy(cxT[:, :], PT[:, :]).then_inc(s_cxT, 1)

            def b_ffn(g):
                act.wait_ge(s_T3, g + 1)
                nc.scalar.copy(xT3[:, :], PT[:, :]).then_inc(s_xT3, 1)

            def b_gelu(g):
                act.wait_ge(s_FF, g + 1)
                act.wait_ge(s_gl, g)
                nc.scalar.activation(yh[:, :], PB[:, :], ACT.Copy, scale=0.5).then_inc(s_yh, 1)
                act.wait_ge(s_yh, g + 1)
                nc.scalar.activation(ysq[:, :], yh[:, :], ACT.Square).then_inc(s_ysq, 1)

            def b_gelu2(g):
                act.wait_ge(s_yv, g + 1)
                nc.scalar.activation(yt[:, :], yv[:, :], ACT.Tanh).then_inc(s_yt, 1)

            act.wait_ge(consts, 9)
            act.wait_ge(derived, 1)
            a_features(0)
            a_silu(0)
            a_keys(0)
            a_proj(0)
            a_log(0)
            a_decays(0)
            a_aug(0)
            a_square(0)
            a_values(0)

            def body(g, more):
                if more:
                    a_features(g + 1)
                b_queries(g)
                if more:
                    a_silu(g + 1)
                    a_keys(g + 1)
                b_exp(g, 0)
                if more:
                    a_proj(g + 1)
                    a_log(g + 1)
                b_exp(g, 1)
                b_probs(g, 0)
                if more:
                    a_decays(g + 1)
                b_exp(g, 2)
                b_probs(g, 1)
                b_exp(g, 3)
                b_probs(g, 2)
                if more:
                    a_aug(g + 1)
                b_probs(g, 3)
                if more:
                    a_square(g + 1)
                b_out(g)
                if more:
                    a_values(g + 1)
                b_ffn(g)
                b_gelu(g)
                b_gelu2(g)

            body(0, True)
            with act.Fori(1, NG - 2) as g:
                body(g, True)
            body(NG - 2, True)
            body(NG - 1, False)

        @block.vector
        def _(dve):
            def stats(g, n, src, st, mv, s_st, s_mv, s_xn):
                dve.wait_ge(s_xn, g)
                stv = cut(st, TPG, 6)
                for i in range(TPG):
                    last = nc.vector.bn_stats(stv[:, i, :], src(i))
                last.then_inc(s_st, 1)
                dve.wait_ge(s_st, g + 1)
                bear(n)
                for i in range(TPG):
                    last = nc.vector.bn_aggr(mv[:, 2 * i:2 * i + 2], stv[:, i, :])
                last.then_inc(s_mv, 1)

            def a_stats(g):
                stats(g, 0, lambda i: x_all[:, bass.ds((TPG * g + i) * E, E)], st1, mv1, s_st1, s_mv1, s_xn1)

            def a_norm(g):
                dve.wait_ge(s_rs1, g + 1)
                dve.wait_ge(s_xT, g)
                for i in range(TPG):
                    last = nc.vector.tensor_scalar(xn1[:, E * i:E * i + E], x_all[:, bass.ds((TPG * g + i) * E, E)],
                                                   mv1[:, 2 * i:2 * i + 1], rs1[:, i:i + 1],
                                                   ALU.subtract, ALU.mult)
                last.then_inc(s_xn1, 1)

            def a_conv(g):
                yv_ = cut(y, SEQ, L)
                dve.wait_ge(s_xpad, g + 1)
                nc.vector.tensor_scalar(yv_, xpad_v[:, :, 0:L], conv_half[:, 0:1], None, ALU.mult).then_inc(s_conv, 1)
                for k in range(1, TAPS):
                    dve.wait_ge(s_conv, TAPS * g + k)
                    nc.vector.scalar_tensor_tensor(out=yv_, in0=xpad_v[:, :, k:k + L], scalar=conv_half[:, k:k + 1],
                                                   in1=yv_, op0=ALU.mult, op1=ALU.add).then_inc(s_conv, 1)

            def a_silu(g):
                dve.wait_ge(s_th1, g + 1)
                dve.wait_ge(s_Gt, g)
                nc.vector.scalar_tensor_tensor(out=xcT[:, :], in0=th1[:, :], scalar=1.0, in1=y[:, :],
                                               op0=ALU.add, op1=ALU.mult).then_inc(s_xc, 1)

            def a_gate(g):
                dve.wait_ge(s_tg, g + 1)
                dve.wait_ge(s_og, g)
                nc.vector.scalar_tensor_tensor(out=sg[:, :], in0=tg[:, :], scalar=1.0, in1=gh[:, :],
                                               op0=ALU.add, op1=ALU.mult).then_inc(s_sg, 1)

            def a_decays(g):
                dve.wait_ge(s_ln, g + 1)
                dve.wait_ge(s_decay, g)
                nc.vector.scalar_tensor_tensor(out=lsig[:, :], in0=kg_s, scalar=0.0, in1=ln1p[:, :],
                                               op0=ALU.min, op1=ALU.subtract).then_inc(s_lsig, 1)
                dve.wait_ge(s_lsig, g + 1)
                nc.vector.tensor_scalar(lclip[:, :], lsig[:, :], LEAST_LOG, None, ALU.max).then_inc(s_lclip, 1)
                dve.wait_ge(s_lclip, g + 1)
                nc.vector.tensor_tensor_scan(G[:, :], carry[:, :], lclip[:, :], 0.0, ALU.mult, ALU.add).then_inc(s_G, 1)
                dve.wait_ge(s_G, g + 1)
                Gv = cut(G, TPG * NCH, CH)
                ref = cut(G, TPG, NCH, CH)[:, :, :, REF]
                dve.wait_ge(s_ek, g)
                nc.vector.tensor_tensor(cut(dq, TPG * NCH, CH), Gv,
                                        Gv[:, :, REF:REF + 1].to_broadcast([P, TPG * NCH, CH]),
                                        ALU.subtract).then_inc(s_dq, 1)
                nc.vector.tensor_tensor(cut(dr, TPG, NCH, NCH), ref.unsqueeze(3).to_broadcast([P, TPG, NCH, NCH]),
                                        ref.unsqueeze(2).to_broadcast([P, TPG, NCH, NCH]),
                                        ALU.subtract).then_inc(s_dr, 1)
                dve.wait_ge(s_dr, g + 1)
                dve.wait_ge(s_er, g)
                nc.vector.tensor_scalar(drc[:, :], dr[:, :], 0.0, None, ALU.min).then_inc(s_drc, 1)
                dve.wait_ge(s_decay, g + 1)
                nc.vector.tensor_scalar(key[:, :], decay[:, :], -1.0, 1.0, ALU.mult, ALU.add).then_inc(s_key, 1)

            def a_keys(g):
                dve.wait_ge(s_key, g + 1)
                dve.wait_ge(s_AUG, g)
                nc.vector.tensor_tensor(qkp[:, :], q_s, key[:, :], ALU.mult).then_inc(s_qkp, 1)
                dve.wait_ge(s_eq, g + 1)
                dve.wait_ge(s_qbd, 16 * NB * g)
                nc.vector.scalar_tensor_tensor(out=qs[:, :], in0=q_s, scalar=float(DKH) ** -0.5, in1=e_q[:, :],
                                               op0=ALU.mult, op1=ALU.mult).then_inc(s_qs, 1)
                dve.wait_ge(s_ek, g + 1)
                dve.wait_ge(s_kc, TPG * g)
                nc.vector.tensor_tensor(ke[:, :], key[:, :], e_k[:, :], ALU.mult).then_inc(s_ke, 1)

            def a_mask(g, j):
                dve.wait_ge(s_AT, 2 * g + j + 1)
                dve.wait_ge(s_AV, 2 * g)
                bear(3 + j)
                mask = cut(causal, NCH, CH).unsqueeze(2).to_broadcast([P, NCH, NB, CH])
                nc.vector.copy_predicated(at_c[:, j, :, :, :], mask, cut(AT, NCH, NB, CH)).then_inc(s_at, 1)

            def a_aug(g):
                dve.wait_ge(s_AUG, g + 1)
                dve.wait_ge(s_vt, g + 1)
                dve.wait_ge(s_tz, g)
                nc.vector.tensor_tensor(cut(z, TPG * H, DVH),
                                        PA0[:, 0:TPG * H].unsqueeze(2).to_broadcast([P, TPG * H, DVH]),
                                        cut(vt, TPG * H, DVH), ALU.mult).then_inc(s_z, 1)

            def a_center(g):
                dve.wait_ge(s_tz, g + 1)
                dve.wait_ge(s_AV, 2 * g + 2)
                nc.vector.scalar_tensor_tensor(out=o_s[:, :], in0=tz[:, :], scalar=0.5, in1=PA1[:, :],
                                               op0=ALU.mult, op1=ALU.add).then_inc(s_o, 1)
                dve.wait_ge(s_o, g + 1)
                nc.vector.tensor_reduce(osum[:, :], cut(o_s, TPG * H, DVH), AX.X, ALU.add).then_inc(s_osum, 1)
                dve.wait_ge(s_osum, g + 1)
                nc.vector.tensor_scalar(omean[:, :], osum[:, :], 1.0 / DVH, None, ALU.mult).then_inc(s_omean, 1)
                dve.wait_ge(s_omean, g + 1)
                dve.wait_ge(s_on, g)
                nc.vector.tensor_tensor(cut(dev, TPG * H, DVH), cut(o_s, TPG * H, DVH),
                                        omean[:, :].unsqueeze(2).to_broadcast([P, TPG * H, DVH]),
                                        ALU.subtract).then_inc(s_dev, 1)

            def a_squares(g):
                dve.wait_ge(s_sq1, g + 1)
                nc.vector.tensor_reduce(oss[:, :], cut(sq1, TPG * H, DVH), AX.X, ALU.add).then_inc(s_oss, 1)
                dve.wait_ge(s_oss, g + 1)
                dve.wait_ge(s_ors, g)
                nc.vector.tensor_scalar(ove[:, :], oss[:, :], 1.0 / DVH, EPS, ALU.mult, ALU.add).then_inc(s_ove, 1)

            def a_gated(g):
                dve.wait_ge(s_OT, g + 1)
                dve.wait_ge(s_sg, g + 1)
                dve.wait_ge(s_Y, g)
                nc.vector.tensor_tensor(ogT[:, :], PA0[:, :], sg[:, :], ALU.mult).then_inc(s_og, 1)

            def a_residual(g):
                dve.wait_ge(s_Y, g + 1)
                dve.wait_ge(s_xn2, g)
                nc.vector.tensor_tensor(x1[:, :], PA1[:, :], x_all[:, bass.ds(g * GT, GT)], ALU.add).then_inc(s_x1, 1)

            def b_stats2(g):
                dve.wait_ge(s_x1, g + 1)
                stats(g, 1, lambda i: x1[:, E * i:E * i + E], st2, mv2, s_st2, s_mv2, s_xn2)

            def b_max(g, i):
                dve.wait_ge(s_S, TPG * g + i + 1)
                dve.wait_ge(s_fold, TPG * g + i)
                nc.vector.tensor_reduce(nmax[:, :], cut(S, XH, L), AX.X, ALU.max, negate=True).then_inc(s_max, 1)

            def b_probs(g, i):
                dve.wait_ge(s_PT, 2 * (TPG * g + i) + 1)
                dve.wait_ge(s_PV, TPG * g + i)
                nc.vector.tensor_copy(prT[:, 0:512], PT[:, :]).then_inc(s_prT, 1)

            def b_weigh(g, i):
                dve.wait_ge(s_PV, TPG * g + i + 1)
                pv = PB[:, 0:XH * VC].rearrange("p (h v) -> p h v", h=XH)
                nc.vector.reciprocal(rden[:, :].unsqueeze(2), pv[:, :, XD:VC]).then_inc(s_rden, 1)
                dve.wait_ge(s_rden, TPG * g + i + 1)
                if i == 0:
                    dve.wait_ge(s_CX, g)
                nc.vector.tensor_tensor(cx[:, E * i:E * i + E].rearrange("p (h v) -> p h v", h=XH), pv[:, :, 0:XD],
                                        rden[:, :].unsqueeze(2).to_broadcast([P, XH, XD]),
                                        ALU.mult).then_inc(s_cx, 1)

            def b_residual(g):
                dve.wait_ge(s_WO, g + 1)
                nc.vector.tensor_tensor(x2[:, :], PB[:, :], x1[:, :], ALU.add).then_inc(s_x2, 1)
                dve.wait_ge(s_x2, g + 1)
                stats(g, 2, lambda i: x2[:, E * i:E * i + E], st3, mv3, s_st3, s_mv3, s_xn3)

            def b_route(g):
                dve.wait_ge(s_RT, g + 1)
                nc.vector.tensor_copy(rs_all[:, :], PT[:, 0:KH]).then_inc(s_rall, 1)
                dve.wait_ge(s_rall, g + 1)
                alls = cut(rs_all, TPG, L)
                nc.vector.tensor_tensor(cut(own, TPG, L), alls, same[:, :].unsqueeze(1).to_broadcast([P, TPG, L]),
                                        ALU.mult).then_inc(s_own, 1)
                dve.wait_ge(s_own, g + 1)
                nc.vector.tensor_reduce(r_own[:, :], cut(own, TPG, L), AX.X, ALU.add).then_inc(s_rown, 1)
                dve.wait_ge(s_rown, g + 1)
                mine = r_own[:, :].unsqueeze(2).to_broadcast([P, TPG, L])
                nc.vector.tensor_tensor(cut(above, TPG, L), alls, mine, ALU.is_gt).then_inc(s_above, 1)
                nc.vector.tensor_tensor(cut(tied, TPG, L), alls, mine, ALU.is_equal).then_inc(s_tied, 1)
                dve.wait_ge(s_tied, g + 1)
                nc.vector.tensor_tensor(cut(tiedb, TPG, L), cut(tied, TPG, L),
                                        before[:, :].unsqueeze(1).to_broadcast([P, TPG, L]),
                                        ALU.mult).then_inc(s_tiedb, 1)
                dve.wait_ge(s_tiedb, g + 1)
                nc.vector.tensor_tensor(cnt[:, :], above[:, :], tiedb[:, :], ALU.add).then_inc(s_cnt, 1)
                dve.wait_ge(s_cnt, g + 1)
                nc.vector.tensor_reduce(rank[:, :], cut(cnt, TPG, L), AX.X, ALU.add).then_inc(s_rank, 1)
                dve.wait_ge(s_rank, g + 1)
                nc.vector.tensor_scalar(taken[:, :], rank[:, :], float(KEEP), None, ALU.is_lt).then_inc(s_taken, 1)

            def b_gelu(g):
                dve.wait_ge(s_ysq, g + 1)
                nc.vector.tensor_scalar(yu[:, :], ysq[:, :], 8.0 * GELU_A * GELU_C, 2.0 * GELU_C, ALU.mult,
                                        ALU.add).then_inc(s_yu, 1)
                dve.wait_ge(s_yu, g + 1)
                nc.vector.tensor_tensor(yv[:, :], yu[:, :], yh[:, :], ALU.mult).then_inc(s_yv, 1)

            def b_result(g):
                dve.wait_ge(s_yt, g + 1)
                nc.vector.scalar_tensor_tensor(out=gl[:, :], in0=yt[:, :], scalar=1.0, in1=yh[:, :],
                                               op0=ALU.add, op1=ALU.mult).then_inc(s_gl, 1)
                dve.wait_ge(s_gl, g + 1)
                dve.wait_ge(s_taken, g + 1)
                dve.wait_ge(s_xn3, g + 1)
                bear(5)
                take = taken[:, :].bitcast(u32).unsqueeze(2).to_broadcast([P, TPG, E])
                nc.vector.copy_predicated(cut(xn3, TPG, E), take, cut(gl, TPG, E)).then_inc(s_sel, 1)
                dve.wait_ge(s_sel, g + 1)
                dve.wait_ge(s_out, 16 * g)
                nc.vector.tensor_tensor(yout[:, :], xn3[:, :], x2[:, :], ALU.add).then_inc(s_yout, 1)

            nc.vector.memset(bearer[:, :], 0.0).then_inc(clear, 1)
            dve.wait_ge(clear, 1)
            dve.wait_ge(x_in, 16)
            a_stats(0)
            a_norm(0)
            nc.vector.memset(k_bd[:, :], 0.0).then_inc(clear, 1)
            nc.vector.memset(v_bd[:, :], 0.0)
            nc.vector.memset(at[:, :], 0.0)
            nc.vector.memset(v_x[:, :], 0.0).then_inc(clear, 1)
            dve.wait_ge(clear, 3)
            for half in range(2):
                ones = v_x[L * half:L * half + L, :].rearrange("p (b q u v) -> p b q u v", b=SEQ, q=PAIRS, u=2)
                nc.vector.memset(ones[:, :, :, half, XD:VC].rearrange("p b q v -> p (b q) v"), 1.0)
            dve.wait_ge(w_in, W_IN)
            dve.wait_ge(consts2, 10)
            nc.vector.tensor_copy(ident_b[:, :], ident[:, :])
            nc.vector.tensor_copy(causal[:, :], causal_f[:, :])
            nc.vector.tensor_scalar(conv_half[:, :], conv_s[:, :], 0.5, None, ALU.mult)
            nc.vector.tensor_scalar(bg_half[:, :], bg_s[:, :], 0.5, None, ALU.mult)
            nc.vector.tensor_scalar(aug_sel[:, :], block_of[:, :], aug_s[:, 0:1], None, ALU.mult)
            nc.vector.tensor_copy(wr_rep[:, :], wr_s[:, 0:1].to_broadcast([P, L])).then_inc(derived, 1)
            dve.wait_ge(derived, 1)
            a_conv(0)
            a_silu(0)
            a_gate(0)
            a_decays(0)
            a_keys(0)
            dve.wait_ge(x_rest, 16)
            a_stats(1)
            a_aug(0)
            a_norm(1)
            a_mask(0, 0)
            a_mask(0, 1)
            a_center(0)
            a_squares(0)
            a_gated(0)
            a_residual(0)
            b_stats2(0)

            def body(g, more, third=True):
                if more:
                    a_conv(g + 1)
                b_max(g, 0)
                if more:
                    a_silu(g + 1)
                    a_gate(g + 1)
                b_max(g, 1)
                b_probs(g, 0)
                if more:
                    a_decays(g + 1)
                b_weigh(g, 0)
                if more:
                    a_keys(g + 1)
                b_max(g, 2)
                b_probs(g, 1)
                b_weigh(g, 1)
                if more:
                    a_aug(g + 1)
                    if third:
                        a_stats(g + 2)
                b_max(g, 3)
                if more:
                    a_mask(g + 1, 0)
                b_probs(g, 2)
                b_weigh(g, 2)
                if more:
                    if third:
                        a_norm(g + 2)
                    a_mask(g + 1, 1)
                b_probs(g, 3)
                b_weigh(g, 3)
                if more:
                    a_center(g + 1)
                    a_squares(g + 1)
                b_residual(g)
                if more:
                    a_gated(g + 1)
                b_route(g)
                b_gelu(g)
                if more:
                    a_residual(g + 1)
                    b_stats2(g + 1)
                b_result(g)

            body(0, True)
            with dve.Fori(1, NG - 2) as g:
                body(g, True)
            body(NG - 2, True, third=False)
            body(NG - 1, False)


_SHAPE = (64, 64, 128)


def kernel(x, ctx_1024, mask_1_bf0, L0_attn_conv_w, L0_attn_wq, L0_attn_wkg, L0_attn_wv, L0_attn_wg, L0_attn_bg,
           L0_attn_wout, L0_attn_aug_balance, L0_xattn_Wq, L0_xattn_Wk, L0_xattn_Wv, L0_xattn_Wo,
           L0_ffn_w_router, L0_ffn_w_block):
    import numpy as np
    import concourse.bacc as bacc
    from concourse.bass_utils import run_bass_kernel_spmd

    ins = {
        "x": x, "ctx": ctx_1024, "conv_w": L0_attn_conv_w, "wq": L0_attn_wq, "wkg": L0_attn_wkg,
        "wv": L0_attn_wv, "wg": L0_attn_wg, "bg": np.asarray(L0_attn_bg)[:, None], "wout": L0_attn_wout,
        "aug": np.asarray(L0_attn_aug_balance)[:, None], "WqT": np.asarray(L0_xattn_Wq).T,
        "WkT": np.asarray(L0_xattn_Wk).T, "WvT": np.asarray(L0_xattn_Wv).T, "WoT": np.asarray(L0_xattn_Wo).T,
        "w_router": np.asarray(L0_ffn_w_router)[:, None], "w_block": L0_ffn_w_block,
    }
    nc = bacc.Bacc("TRN2", target_bir_lowering=False, num_devices=1)
    arrays, args = {}, []
    for name, a in ins.items():
        a = np.ascontiguousarray(a)
        arrays[f"in_{name}"] = a
        args.append(nc.dram_tensor(f"in_{name}", a.shape, mybir.dt.from_np(a.dtype), kind="ExternalInput").ap())
    args.append(nc.dram_tensor("out_0", _SHAPE, mybir.dt.float32, kind="ExternalOutput").ap())
    decoder_layer(nc, *args)
    r = run_bass_kernel_spmd(nc, [arrays], core_ids=[0])
    return r.results[0]["out_0"]
```

```python
import concourse.bass as bass
from concourse import mybir
from contextlib import ExitStack


def decoder_layer(
    nc: bass.Bass,
    x: bass.AP, ctx_in: bass.AP, conv_w: bass.AP, wq: bass.AP, wkg: bass.AP, wv: bass.AP, wg: bass.AP,
    bg: bass.AP, wout: bass.AP, aug: bass.AP, WqT: bass.AP, WkT: bass.AP, WvT: bass.AP, WoT: bass.AP,
    w_router: bass.AP, w_block: bass.AP, out: bass.AP,
):
    fp32 = mybir.dt.float32
    bf16 = mybir.dt.bfloat16
    u32 = mybir.dt.uint32
    ALU = mybir.AluOpType
    ACT = mybir.ActivationFunctionType
    AX = mybir.AxisListType

    B, L, E = x.shape
    P = 128
    TPG = 4
    NT = B * L // P
    NG = NT // TPG
    GT = TPG * P
    SEQ = GT // L
    DK = wq.shape[1]
    H = 8
    DKH, DVH = DK // H, E // H
    XH = 16
    XD = E // XH
    NB = 2 * H
    KH = TPG * L
    TAPS = conv_w.shape[1]
    PADL = TAPS - 1 + L
    CH = 8
    NCH = L // CH
    REF = CH // 2 - 1
    NORMALIZER = 16.0
    LEAST_LOG = -20.0 * NORMALIZER
    EPS = 1e-5
    KEEP = max(1, int(L * 0.75))
    GELU_C, GELU_A = 0.7978845608028654, 0.044715
    PAIRS = XH // 2
    VC = XD + 1

    x_tiles = x.rearrange("b l e -> (b l) e").rearrange("(t p) e -> p t e", p=P)
    ctx_tiles = ctx_in.rearrange("b l e -> (b l) e").rearrange("(t p) e -> p t e", p=P)
    out_tiles = out.rearrange("b l e -> (b l) e").rearrange("(t p) e -> p t e", p=P)

    stack = ExitStack()
    with stack:
        def sb(name, cols, dt=fp32, parts=P):
            return stack.enter_context(nc.sbuf_tensor(name, [parts, cols], dt))

        def sem(name):
            return stack.enter_context(nc.semaphore(name))

        def cut(t, *dims):
            a = t[:, :]
            names = "abcd"[:len(dims)]
            return a.rearrange(f"p ({' '.join(names)}) -> p {' '.join(names)}",
                               **{n: d for n, d in zip(names, dims)})

        ident = sb("ident", P)
        ident_b = sb("ident_b", P, bf16)
        causal = sb("causal", L, u32)
        causal_f = sb("causal_f", L)
        before = sb("before", L)
        same = sb("same", L)
        block_of = sb("block_of", NB)
        aug_sel = sb("aug_sel", NB)
        carry = sb("carry", KH)
        minus_half = sb("minus_half", TPG * H)
        eps_s = sb("eps_s", TPG)
        bearer = sb("bearer", 7)
        wq_s, wkg_s = sb("wq_s", DK), sb("wkg_s", DK)
        wv_s, wg_s, wout_s = sb("wv_s", E), sb("wg_s", E), sb("wout_s", E)
        WqT_s, WkT_s, WvT_s, WoT_s = sb("WqT_s", E), sb("WkT_s", E), sb("WvT_s", E), sb("WoT_s", E)
        wblk_s = sb("wblk_s", E)
        wr_s = sb("wr_s", 1)
        wr_rep = sb("wr_rep", L)
        conv_s, bg_s, aug_s = sb("conv_s", TAPS), sb("bg_s", 1), sb("aug_s", 1)
        conv_half, bg_half = sb("conv_half", TAPS), sb("bg_half", 1)

        x_all = sb("x_all", NT * E)
        xa = cut(x_all, NT, E)
        st1, mv1, ve1, rs1 = sb("st1", TPG * 6), sb("mv1", TPG * 2), sb("ve1", TPG), sb("rs1", TPG)
        xn1 = sb("xn1", GT)
        xpad = sb("xpad", SEQ * PADL)
        xpad_v = cut(xpad, SEQ, PADL)
        y = sb("y", GT)
        th1 = sb("th1", GT)
        xcT = sb("xcT", GT)
        qk = sb("qk", 2 * KH)
        q_s, kg_s = qk[:, 0:KH], qk[:, KH:2 * KH]
        ab, ex, ln1p, lsig = sb("ab", KH), sb("ex", KH), sb("ln1p", KH), sb("lsig", KH)
        decay, key, lclip, G = sb("decay", KH), sb("key", KH), sb("lclip", KH), sb("G", KH)
        dq, dr = sb("dq", KH), sb("dr", TPG * NCH * NCH)
        drc = sb("drc", TPG * NCH * NCH)
        e_q, e_k, e_r = sb("e_q", KH), sb("e_k", KH), sb("e_r", TPG * NCH * NCH)
        qs, ke, qkp = sb("qs", KH), sb("ke", KH), sb("qkp", KH)
        kc = sb("kc", TPG * NCH * L)
        kc_m = cut(kc, TPG, NCH, L)
        q_bd = sb("q_bd", NB * KH)
        q_bdv = cut(q_bd, NB, KH)
        vt = sb("vt", GT)
        v_bd = sb("v_bd", 2 * 2 * 2 * E)
        v_bdv = v_bd[:, :].rearrange("p (j x w f) -> p j x w f", j=2, x=2, w=2)
        at = sb("at", 2 * NB * L)
        at_m = cut(at, 2, NB, L)
        at_c = at[:, :].rearrange("p (j n c s) -> p j c n s", j=2, n=NB, c=NCH)
        gh, tg, sg = sb("gh", GT), sb("tg", GT), sb("sg", GT)
        z, tz, o_s, dev, sq1, on = (sb(n, GT) for n in ("z", "tz", "o_s", "dev", "sq1", "on"))
        osum, omean, oss, ove, ors = (sb(n, TPG * H) for n in ("osum", "omean", "oss", "ove", "ors"))
        ogT = sb("ogT", GT)
        c_s, cT = sb("c_s", GT), sb("cT", GT)
        kx = sb("kx", GT)
        k_bd = sb("k_bd", XH * GT)
        k_bdv = cut(k_bd, XH, GT)
        v_x = sb("v_x", SEQ * PAIRS * 2 * VC)
        v_xv = cut(v_x, SEQ, PAIRS, 2 * VC)

        st2, mv2, ve2, rs2 = sb("st2", TPG * 6), sb("mv2", TPG * 2), sb("ve2", TPG), sb("rs2", TPG)
        xn2, xT2, qT = sb("xn2", GT), sb("xT2", GT), sb("qT", GT)
        nmax = sb("nmax", XH, bf16)
        pr = sb("pr", 2 * XH * L)
        pr_v = cut(pr, 2, XH * L)
        prT = sb("prT", PAIRS * P)
        prT_v = cut(prT, PAIRS, P)
        rden = sb("rden", XH)
        cx, cxT, x2 = sb("cx", GT), sb("cxT", GT), sb("x2", GT)
        st3, mv3, ve3, rs3 = sb("st3", TPG * 6), sb("mv3", TPG * 2), sb("ve3", TPG), sb("rs3", TPG)
        xn3, xT3 = sb("xn3", GT), sb("xT3", GT)
        yh, ysq, yu, yv, yt, gl = (sb(n, GT) for n in ("yh", "ysq", "yu", "yv", "yt", "gl"))
        rs_all = sb("rs_all", KH)
        own, r_own = sb("own", KH), sb("r_own", TPG)
        above, tied, tiedb, cnt = sb("above", KH), sb("tied", KH), sb("tiedb", KH), sb("cnt", KH)
        rank, taken = sb("rank", TPG), sb("taken", TPG)
        yout = sb("yout", GT)

        def ps(name, cols):
            return stack.enter_context(nc.psum_tensor(name, [P, cols], fp32))

        PA0, PA1, AT = ps("PA0", 512), ps("PA1", 512), ps("AT", 1024)
        S, PT, PB = ps("S", 1024), ps("PT", 512), ps("PB", 512)
        AT0, AT1 = AT[:, 0:512], AT[:, 512:1024]

        w_in, x_in, x_rest, c_in = sem("w_in"), sem("x_in"), sem("x_rest"), sem("c_in")
        consts, consts2, derived = sem("consts"), sem("consts2"), sem("derived")
        q_clear, clear = sem("q_clear"), sem("clear")
        s_st1, s_mv1, s_ve1, s_rs1, s_xn1 = (sem(n) for n in ("s_st1", "s_mv1", "s_ve1", "s_rs1", "s_xn1"))
        s_xT, s_xpad, s_conv, s_th1, s_xc = (sem(n) for n in ("s_xT", "s_xpad", "s_conv", "s_th1", "s_xc"))
        s_QK, s_V, s_Gt, s_qk, s_vt = (sem(n) for n in ("s_QK", "s_V", "s_Gt", "s_qk", "s_vt"))
        s_ab, s_ex, s_ln, s_lsig, s_decay, s_key = (
            sem(n) for n in ("s_ab", "s_ex", "s_ln", "s_lsig", "s_decay", "s_key"))
        s_lclip, s_G, s_dq, s_dr, s_drc = (sem(n) for n in ("s_lclip", "s_G", "s_dq", "s_dr", "s_drc"))
        s_eq, s_ek, s_er, s_qs, s_ke, s_qkp, s_kc = (
            sem(n) for n in ("s_eq", "s_ek", "s_er", "s_qs", "s_ke", "s_qkp", "s_kc"))
        s_qbd, s_vbd = sem("s_qbd"), sem("s_vbd")
        s_AUG, s_AT, s_at, s_AV = (sem(n) for n in ("s_AUG", "s_AT", "s_at", "s_AV"))
        s_gh, s_tg, s_sg = (sem(n) for n in ("s_gh", "s_tg", "s_sg"))
        s_z, s_tz, s_o, s_osum, s_omean, s_dev, s_sq1, s_oss = (
            sem(n) for n in ("s_z", "s_tz", "s_o", "s_osum", "s_omean", "s_dev", "s_sq1", "s_oss"))
        s_ove, s_ors, s_on, s_OT, s_og, s_Y, s_x1 = (
            sem(n) for n in ("s_ove", "s_ors", "s_on", "s_OT", "s_og", "s_Y", "s_x1"))
        s_CT, s_cT, s_KX, s_kx, s_VX, s_vx = (sem(n) for n in ("s_CT", "s_cT", "s_KX", "s_kx", "s_VX", "s_vx"))
        s_kbd = [sem("s_kbd0"), sem("s_kbd1")]
        s_st2, s_mv2, s_ve2, s_rs2, s_xn2 = (sem(n) for n in ("s_st2", "s_mv2", "s_ve2", "s_rs2", "s_xn2"))
        s_T2, s_xT2, s_Q, s_qT = (sem(n) for n in ("s_T2", "s_xT2", "s_Q", "s_qT"))
        s_S, s_max, s_fold, s_exp = (sem(n) for n in ("s_S", "s_max", "s_fold", "s_exp"))
        s_PT, s_prT = sem("s_PT"), sem("s_prT")
        s_PV = sem("s_PV")
        s_rden, s_cx = sem("s_rden"), sem("s_cx")
        s_CX, s_cxT, s_WO, s_x2 = (sem(n) for n in ("s_CX", "s_cxT", "s_WO", "s_x2"))
        s_st3, s_mv3, s_ve3, s_rs3, s_xd3, s_xn3 = (
            sem(n) for n in ("s_st3", "s_mv3", "s_ve3", "s_rs3", "s_xd3", "s_xn3"))
        s_T3, s_xT3, s_FF, s_RT = (sem(n) for n in ("s_T3", "s_xT3", "s_FF", "s_RT"))
        s_yh, s_ysq, s_yu, s_yv, s_yt, s_gl = (sem(n) for n in ("s_yh", "s_ysq", "s_yu", "s_yv", "s_yt", "s_gl"))
        s_rall, s_own, s_rown, s_above, s_tied, s_tiedb, s_cnt, s_rank, s_taken = (
            sem(n) for n in ("s_rall", "s_own", "s_rown", "s_above", "s_tied", "s_tiedb", "s_cnt", "s_rank",
                             "s_taken"))
        s_sel, s_yout, s_out = sem("s_sel"), sem("s_yout"), sem("s_out")

        WEIGHTS = [(wq_s, wq), (wkg_s, wkg), (wv_s, wv), (wg_s, wg), (wout_s, wout), (WqT_s, WqT),
                   (WkT_s, WkT), (WvT_s, WvT), (WoT_s, WoT), (wblk_s, w_block), (conv_s, conv_w),
                   (wr_s, w_router), (bg_s, bg), (aug_s, None)]
        W_IN = 16 * (len(WEIGHTS) + 1)

        def bear(n):
            nc.vector.tensor_copy(bearer[:, 1 + n:2 + n], bearer[:, 0:1])

        def has(g):
            return not isinstance(g, int) or 0 <= g < NG

        def upto(g):
            return min(g, NG) if isinstance(g, int) else g

        FIRST, LAST = 2, NG - 3

        def steps(eng, step):
            for n in range(-2, FIRST):
                step(n)
            with eng.Fori(FIRST, LAST) as n:
                step(n)
            for n in range(LAST, NG + 1):
                step(n)

        block = stack.enter_context(nc.Block())

        @block.sync
        def _(sp):
            def held(v):
                return v if isinstance(v, int) else sp.to_reg(v)

            def load_ctx(g):
                sp.wait_ge(s_CT, g)
                sp.dma_start(cut(c_s, TPG, E), ctx_tiles[:, bass.ds(TPG * g, TPG), :]).then_inc(c_in, 16)

            def queries_to_blocks(g):
                scaled, scored = held(g + 1), held(2 * g)
                sp.wait_ge(s_qs, scaled)
                sp.wait_ge(s_AT, scored)
                for n in range(NB):
                    sp.dma_start(q_bdv[8 * n:8 * n + 8, n, :], qs[8 * n:8 * n + 8, :]).then_inc(s_qbd, 16)

            def values_to_blocks(g):
                copied, used = held(g + 1), held(2 * g)
                sp.wait_ge(s_vt, copied)
                sp.wait_ge(s_AV, used)
                for half in range(2):
                    for w in range(2):
                        src = vt[L * half:L * half + L, :].rearrange("p (j w f) -> p j w f", j=2, w=2)[:, :, w, :]
                        sp.dma_start(v_bdv[L * w:L * w + L, :, half, w, :], src).then_inc(s_vbd, 16)

            def keys_to_blocks(g, part):
                copied = held(g + 1)
                if not isinstance(g, int) or g > 0:
                    scored = held(TPG * g - 2 + 2 * part)
                    sp.wait_ge(s_S, scored)
                sp.wait_ge(s_kx, copied)
                cols = slice(GT // 2 * part, GT // 2 * part + GT // 2)
                for h in range(XH):
                    sp.dma_start(k_bdv[8 * h:8 * h + 8, h, cols], kx[8 * h:8 * h + 8, cols]).then_inc(s_kbd[part], 16)

            def store(g):
                ready = held(g + 1)
                sp.wait_ge(s_yout, ready)
                sp.dma_start(out_tiles[:, bass.ds(TPG * g, TPG), :], cut(yout, TPG, E)).then_inc(s_out, 16)

            sp.dma_start(xa[:, 0:TPG, :], x_tiles[:, 0:TPG, :]).then_inc(x_in, 16)
            for dst, src in WEIGHTS[:-1]:
                sp.dma_start(dst[:, :], src).then_inc(w_in, 16)
            for half in range(2):
                sp.dma_start(aug_s[DK * half:DK * half + DK, :], aug).then_inc(w_in, 16)
            sp.dma_start(xa[:, TPG:NT, :], x_tiles[:, TPG:NT, :]).then_inc(x_rest, 16)
            sp.wait_ge(clear, 3)
            sp.wait_ge(q_clear, 1)

            def step(n):
                a, b, c = n + 2, n + 1, n - 1
                if has(b + 1):
                    load_ctx(b + 1)
                if has(b):
                    keys_to_blocks(b, 0)
                if has(a):
                    values_to_blocks(a)
                    queries_to_blocks(a)
                if has(b):
                    keys_to_blocks(b, 1)
                if has(c):
                    store(c)

            steps(sp, step)
            sp.wait_ge(s_out, 16 * NG)

        @block.gpsimd
        def _(pool):
            nc.gpsimd.memset(ident[:, :], 0.0).then_inc(consts, 1)
            nc.gpsimd.memset(causal_f[:, :], 1.0).then_inc(consts, 1)
            nc.gpsimd.memset(before[:, :], 1.0).then_inc(consts, 1)
            nc.gpsimd.memset(same[:, :], 0.0).then_inc(consts, 1)
            nc.gpsimd.memset(block_of[:, :], 1.0).then_inc(consts, 1)
            nc.gpsimd.memset(carry[:, :], 1.0).then_inc(consts, 1)
            nc.gpsimd.memset(minus_half[:, :], -0.5).then_inc(consts, 1)
            nc.gpsimd.memset(xpad[:, :], 0.0).then_inc(consts, 1)
            nc.gpsimd.memset(eps_s[:, :], EPS).then_inc(consts, 1)
            pool.wait_ge(consts, 9)
            made = 0

            def select(t, keep, fill, base, step, by_row):
                nonlocal made
                nc.gpsimd.affine_select(out=t, in_=t, compare_op=keep, fill=fill, base=base,
                                        pattern=[[step, t.shape[1]]], channel_multiplier=by_row).then_inc(consts2, 1)
                made += 1
                pool.wait_ge(consts2, made)

            select(ident[:, :], ALU.not_equal, 1.0, 0, -1, 1)
            for half in range(2):
                rows = slice(L * half, L * half + L)
                select(causal_f[rows, :], ALU.is_ge, 0.0, 0, 1, -1)
                select(before[rows, :], ALU.is_gt, 0.0, 0, -1, 1)
                select(same[rows, :], ALU.not_equal, 1.0, 0, -1, 1)
            select(block_of[:, :], ALU.is_ge, 0.0, 0, -8, 1)
            select(block_of[:, :], ALU.is_ge, 0.0, 7, 8, -1)
            nc.gpsimd.memset(cut(carry, TPG, L)[:, :, 0:1], 0.0).then_inc(consts2, 1)

            def scales(g, s_mv, s_ve, s_rs, s_xn, mv, ve, rs):
                pool.wait_ge(s_mv, g + 1)
                nc.gpsimd.tensor_tensor(cut(ve, TPG, 1), cut(mv, TPG, 2)[:, :, 1:2], cut(eps_s, TPG, 1),
                                        ALU.add).then_inc(s_ve, 1)
                pool.wait_ge(s_ve, g + 1)
                pool.wait_ge(s_xn, g)
                nc.gpsimd.tensor_tensor(rs[:, :], ve[:, :], minus_half[:, 0:TPG], ALU.pow).then_inc(s_rs, 1)

            def norm(g, s_mv, s_ve, s_rs, s_xd, s_xn, s_read, src, mv, ve, rs, dst):
                scales(g, s_mv, s_ve, s_rs, s_xn, mv, ve, rs)
                for s in s_read:
                    pool.wait_ge(s, g)
                nc.gpsimd.tensor_tensor(cut(dst, TPG, E), cut(src, TPG, E),
                                        cut(mv, TPG, 2)[:, :, 0:1].to_broadcast([P, TPG, E]),
                                        ALU.subtract).then_inc(s_xd, 1)
                pool.wait_ge(s_xd, g + 1)
                pool.wait_ge(s_rs, g + 1)
                nc.gpsimd.tensor_tensor(cut(dst, TPG, E), cut(dst, TPG, E),
                                        rs[:, :].unsqueeze(2).to_broadcast([P, TPG, E]),
                                        ALU.mult).then_inc(s_xn, 1)

            def norm_a(g):
                scales(g, s_mv1, s_ve1, s_rs1, s_xn1, mv1, ve1, rs1)

            def norm_b2(g):
                scales(g, s_mv2, s_ve2, s_rs2, s_xn2, mv2, ve2, rs2)

            def norm_b3(g):
                norm(g, s_mv3, s_ve3, s_rs3, s_xd3, s_xn3, [s_T3, s_yout], x2, mv3, ve3, rs3, xn3)

            def keys(g):
                pool.wait_ge(s_ke, g + 1)
                pool.wait_ge(s_er, g + 1)
                pool.wait_ge(s_AT, 2 * g)
                kev = cut(ke, TPG, NCH, CH)
                erv = cut(e_r, TPG, NCH, NCH)
                for i in range(TPG):
                    nc.gpsimd.tensor_tensor(
                        kc[:, i * NCH * L:(i + 1) * NCH * L].rearrange(
                            "p (c d s) -> p c d s", c=NCH, d=NCH),
                        kev[:, i, :, :].unsqueeze(1).to_broadcast([P, NCH, NCH, CH]),
                        erv[:, i, :, :].unsqueeze(3).to_broadcast([P, NCH, NCH, CH]), ALU.mult).then_inc(s_kc, 1)

            def group_norm(g):
                pool.wait_ge(s_ove, g + 1)
                nc.gpsimd.tensor_tensor(ors[:, :], ove[:, :], minus_half[:, :], ALU.pow).then_inc(s_ors, 1)
                pool.wait_ge(s_ors, g + 1)
                pool.wait_ge(s_OT, g)
                nc.gpsimd.tensor_tensor(cut(on, TPG * H, DVH), cut(dev, TPG * H, DVH),
                                        ors[:, :].unsqueeze(2).to_broadcast([P, TPG * H, DVH]),
                                        ALU.mult).then_inc(s_on, 1)

            norm_a(0)
            nc.gpsimd.memset(q_bd[:, :], 0.0).then_inc(q_clear, 1)

            def step(n):
                a, b, c = n + 2, n + 1, n - 1
                if has(c):
                    norm_b3(c)
                if has(b):
                    group_norm(b)
                if has(a):
                    keys(a)
                if has(b):
                    norm_b2(b)
                if has(a + 1):
                    norm_a(a + 1)

            steps(pool, step)

        @block.tensor
        def _(pe):
            def to_features(dst, src):
                for i in range(TPG):
                    last = nc.tensor.transpose(dst[:, P * i:P * i + P], src[:, P * i:P * i + P], ident[:, :])
                return last

            def transpose_x(g):
                pe.wait_ge(s_xn1, g + 1)
                pe.wait_ge(s_z, g)
                to_features(PA0, xn1).then_inc(s_xT, 1)

            def transpose_ctx(g):
                pe.wait_ge(c_in, 16 * (g + 1))
                pe.wait_ge(s_o, g + 1)
                to_features(PA1, c_s).then_inc(s_CT, 1)

            def context_keys(g):
                pe.wait_ge(s_cT, g + 1)
                pe.wait_ge(s_at, 2 * (g + 1))
                nc.tensor.matmul(AT1, WkT_s[:, :], cT[:, :], start=True, stop=True).then_inc(s_KX, 1)

            def context_values(g):
                pe.wait_ge(s_cT, g + 1)
                pe.wait_ge(s_exp, TPG * g)
                for b in range(SEQ):
                    for half in range(2):
                        last = nc.tensor.matmul(S[L * half:L * half + L, E * b:E * b + E], cT[:, L * b:L * b + L],
                                                WvT_s[:, :], start=True, stop=True)
                last.then_inc(s_VX, 1)

            def project(g):
                xc_h = xcT[:, :].rearrange("p (i x t) -> p i x t", i=TPG, x=2)
                pe.wait_ge(s_xc, g + 1)
                pe.wait_ge(s_xpad, g + 1)
                for n, w in enumerate((wq_s, wkg_s)):
                    for half in range(2):
                        last = nc.tensor.matmul(PA0[L * half:L * half + L, KH * n:KH * n + KH], w[:, :],
                                                xc_h[:, :, half, :], start=True, stop=True)
                last.then_inc(s_QK, 1)
                pe.wait_ge(s_cT, g)
                for i in range(TPG):
                    last = nc.tensor.matmul(PA1[:, E * i:E * i + E], xcT[:, P * i:P * i + P], wv_s[:, :],
                                            start=True, stop=True)
                last.then_inc(s_V, 1)
                pe.wait_ge(s_at, 2 * g)
                nc.tensor.matmul(AT0, wg_s[:, :], xcT[:, :], start=True, stop=True).then_inc(s_Gt, 1)

            def aug_weights(g):
                pe.wait_ge(s_qkp, g + 1)
                pe.wait_ge(s_og, g)
                for i in range(TPG):
                    for half in range(2):
                        last = nc.tensor.matmul(PA0[L * half:L * half + L, H * i:H * i + H],
                                                qkp[:, L * i:L * i + L], aug_sel[:, H * half:H * half + H],
                                                start=True, stop=True)
                last.then_inc(s_AUG, 1)

            def scores(g, j):
                pe.wait_ge(s_kc, TPG * g + 2 * j + 2)
                if j == 0:
                    pe.wait_ge(s_qbd, 16 * NB * (g + 1))
                    pe.wait_ge(s_gh, g + 1)
                    pe.wait_ge(s_kx, g)
                else:
                    pe.wait_ge(s_at, 2 * g + j)
                for c in range(NCH):
                    for w in range(2):
                        i = 2 * j + w
                        last = nc.tensor.matmul(AT[L * w:L * w + L, c * NB * CH:(c + 1) * NB * CH],
                                                kc_m[:, i, c, :],
                                                q_bdv[:, :, L * i + CH * c:L * i + CH * c + CH],
                                                start=True, stop=True)
                last.then_inc(s_AT, 1)

            def attend(g, j, heads=range(H)):
                pe.wait_ge(s_at, 2 * g + j + 1)
                if j == 0 and heads[0] == 0:
                    pe.wait_ge(s_vbd, 64 * (g + 1))
                    pe.wait_ge(s_x1, g)
                o_v = PA1[:, :].rearrange("p (j w f) -> p j w f", j=2, w=2)
                for h in heads:
                    for half in range(2):
                        n = H * half + h
                        last = nc.tensor.matmul(o_v[L * half:L * half + L, j, :, DVH * h:DVH * h + DVH],
                                                at_m[:, j, n, :], v_bdv[:, j, half, :, DVH * h:DVH * h + DVH],
                                                start=True, stop=True)
                if heads[-1] == H - 1:
                    last.then_inc(s_AV, 1)

            def transpose_o(g):
                pe.wait_ge(s_on, g + 1)
                pe.wait_ge(s_qk, upto(g + 2))
                to_features(PA0, on).then_inc(s_OT, 1)

            def gla_out(g):
                pe.wait_ge(s_og, g + 1)
                pe.wait_ge(s_vt, upto(g + 2))
                for i in range(TPG):
                    last = nc.tensor.matmul(PA1[:, E * i:E * i + E], ogT[:, P * i:P * i + P], wout_s[:, :],
                                            start=True, stop=True)
                last.then_inc(s_Y, 1)

            def queries(g):
                pe.wait_ge(s_xn2, g + 1)
                pe.wait_ge(s_cxT, g)
                to_features(PT, xn2).then_inc(s_T2, 1)

            def queries2(g):
                pe.wait_ge(s_xT2, g + 1)
                pe.wait_ge(s_x2, g)
                nc.tensor.matmul(PB[:, :], WqT_s[:, :], xT2[:, :], start=True, stop=True).then_inc(s_Q, 1)

            def x_scores(g, i):
                if i == 0:
                    pe.wait_ge(s_qT, g + 1)
                    pe.wait_ge(s_kbd[0], 16 * XH * (g + 1))
                    pe.wait_ge(s_vx, g + 1)
                else:
                    pe.wait_ge(s_exp, TPG * g + i)
                if i == TPG // 2:
                    pe.wait_ge(s_kbd[1], 16 * XH * (g + 1))
                hh = XH // 2
                for n in range(2):
                    for half in range(2):
                        b = 2 * i + half
                        last = nc.tensor.matmul(S[L * half:L * half + L, 512 * n:512 * n + 512],
                                                qT[:, L * b:L * b + L],
                                                k_bdv[:, hh * n:hh * n + hh, L * b:L * b + L], start=True, stop=False,
                                                skip_group_check=True)
                last.then_inc(s_S, 1)

            def less_max(g, i):
                pe.wait_ge(s_max, TPG * g + i + 1)
                hh = XH // 2
                for n in range(2):
                    last = nc.tensor.matmul(S[:, 512 * n:512 * n + 512], ident_b[:, :],
                                            nmax[:, hh * n:hh * n + hh].unsqueeze(2).to_broadcast([P, hh, L]),
                                            start=False, stop=True, skip_group_check=True)
                last.then_inc(s_fold, 1)

            def x_attend(g, i, n):
                hp = PAIRS // 2
                if n == 0:
                    pe.wait_ge(s_exp, TPG * g + i + 1)
                pe.wait_ge(s_prT, 2 * (TPG * g + i) + n)
                if i == 0 and n == 0:
                    pe.wait_ge(s_rall, g)
                for p in range(hp):
                    last = nc.tensor.transpose(PT[:, P * p:P * p + P],
                                               pr_v[:, i % 2, P * (hp * n + p):P * (hp * n + p) + P], ident[:, :])
                last.then_inc(s_PT, 1)

            def x_values(g, i, n):
                hp = PAIRS // 2
                pe.wait_ge(s_prT, 2 * (TPG * g + i) + n + 1)
                if n == 0:
                    pe.wait_ge(s_cx, TPG * g + i)
                    if i == 0:
                        pe.wait_ge(s_yh, g)
                for p in range(hp * n, hp * n + hp):
                    for half in range(2):
                        last = nc.tensor.matmul(PB[L * half:L * half + L, 2 * VC * p:2 * VC * p + 2 * VC],
                                                prT_v[:, p, L * half:L * half + L], v_xv[:, 2 * i + half, p, :],
                                                start=True, stop=True)
                last.then_inc(s_PV, 1)

            def x_out(g):
                pe.wait_ge(s_cx, TPG * g + TPG)
                pe.wait_ge(s_prT, 2 * TPG * (g + 1))
                to_features(PT, cx).then_inc(s_CX, 1)

            def x_out2(g):
                pe.wait_ge(s_cxT, g + 1)
                for i in range(TPG):
                    last = nc.tensor.matmul(PB[:, E * i:E * i + E], cxT[:, P * i:P * i + P], WoT_s[:, :],
                                            start=True, stop=True)
                last.then_inc(s_WO, 1)

            def transpose_x2(g):
                pe.wait_ge(s_xn3, g + 1)
                pe.wait_ge(s_xT2, upto(g + 2))
                to_features(PT, xn3).then_inc(s_T3, 1)

            def ffn(g):
                pe.wait_ge(s_xT3, g + 1)
                x_h = xT3[:, :].rearrange("p (i x t) -> p i x t", i=TPG, x=2)
                for half in range(2):
                    last = nc.tensor.matmul(PT[L * half:L * half + L, 0:KH], wr_rep[:, :], x_h[:, :, half, :],
                                            start=True, stop=True)
                last.then_inc(s_RT, 1)
                pe.wait_ge(s_qT, upto(g + 2))
                for i in range(TPG):
                    last = nc.tensor.matmul(PB[:, E * i:E * i + E], xT3[:, P * i:P * i + P], wblk_s[:, :],
                                            start=True, stop=True)
                last.then_inc(s_FF, 1)

            pe.wait_ge(w_in, W_IN)
            pe.wait_ge(consts2, 10)
            pe.wait_ge(derived, 1)

            def step(n):
                a, b, c = n + 2, n + 1, n - 1
                A, B_, N, C = has(a), has(b), has(n), has(c)
                if B_:
                    attend(b, 1, range(H // 2))
                if N:
                    x_scores(n, 0)
                if B_:
                    attend(b, 1, range(H // 2, H))
                if N:
                    less_max(n, 0)
                if A:
                    transpose_x(a)
                if C:
                    transpose_x2(c)
                if N:
                    x_scores(n, 1)
                if B_:
                    transpose_ctx(b)
                if C:
                    ffn(c)
                if N:
                    less_max(n, 1)
                    x_attend(n, 0, 0)
                if B_:
                    context_keys(b)
                if N:
                    x_scores(n, 2)
                    x_attend(n, 0, 1)
                    x_values(n, 0, 0)
                    less_max(n, 2)
                    x_attend(n, 1, 0)
                    x_values(n, 0, 1)
                if A:
                    project(a)
                if N:
                    x_scores(n, 3)
                    x_attend(n, 1, 1)
                    x_values(n, 1, 0)
                    less_max(n, 3)
                    x_attend(n, 2, 0)
                    x_values(n, 1, 1)
                if B_:
                    transpose_o(b)
                if N:
                    x_attend(n, 2, 1)
                    x_values(n, 2, 0)
                if B_:
                    context_values(b)
                    gla_out(b)
                if N:
                    x_attend(n, 3, 0)
                    x_values(n, 2, 1)
                if A:
                    aug_weights(a)
                if N:
                    x_attend(n, 3, 1)
                    x_values(n, 3, 0)
                if A:
                    scores(a, 0)
                if N:
                    x_values(n, 3, 1)
                if A:
                    scores(a, 1)
                if N:
                    x_out(n)
                if A:
                    attend(a, 0)
                if N:
                    x_out2(n)
                if B_:
                    queries(b)
                    queries2(b)

            steps(pe, step)

        @block.scalar
        def _(act):
            def a_features(g):
                act.wait_ge(s_xT, g + 1)
                act.wait_ge(s_conv, TAPS * g)
                nc.scalar.copy(xpad_v[:, :, TAPS - 1:PADL], cut(PA0, SEQ, L)).then_inc(s_xpad, 1)

            def a_context(g):
                act.wait_ge(s_CT, g + 1)
                act.wait_ge(s_VX, g)
                nc.scalar.copy(cT[:, :], PA1[:, :]).then_inc(s_cT, 1)

            def a_silu(g):
                act.wait_ge(s_conv, TAPS * (g + 1))
                nc.scalar.activation(th1[:, :], y[:, :], ACT.Tanh).then_inc(s_th1, 1)

            def a_keys(g):
                act.wait_ge(s_KX, g + 1)
                act.wait_ge(s_kbd[0], 16 * XH * g)
                act.wait_ge(s_kbd[1], 16 * XH * g)
                nc.scalar.copy(kx[:, :], AT1).then_inc(s_kx, 1)

            def a_proj(g):
                act.wait_ge(s_QK, g + 1)
                act.wait_ge(s_qkp, g)
                nc.scalar.copy(qk[:, :], PA0[:, :]).then_inc(s_qk, 1)
                act.wait_ge(s_Gt, g + 1)
                act.wait_ge(s_sg, g)
                nc.scalar.activation(gh[:, :], AT0, ACT.Identity, bias=bg_half[:, :], scale=0.5).then_inc(s_gh, 1)
                act.wait_ge(s_V, g + 1)
                act.wait_ge(s_vbd, 64 * g)
                act.wait_ge(s_z, g)
                nc.scalar.copy(vt[:, :], PA1[:, :]).then_inc(s_vt, 1)

            def a_gate(g):
                act.wait_ge(s_gh, g + 1)
                nc.scalar.activation(tg[:, :], gh[:, :], ACT.Tanh).then_inc(s_tg, 1)

            def a_log(g):
                act.wait_ge(s_qk, g + 1)
                nc.scalar.activation(ab[:, :], kg_s, ACT.Abs).then_inc(s_ab, 1)
                act.wait_ge(s_ab, g + 1)
                nc.scalar.activation(ex[:, :], ab[:, :], ACT.Exp, scale=-1.0).then_inc(s_ex, 1)
                act.wait_ge(s_ex, g + 1)
                act.wait_ge(s_lsig, g)
                nc.scalar.activation(ln1p[:, :], ex[:, :], ACT.Ln, bias=1.0).then_inc(s_ln, 1)

            def a_decays(g):
                act.wait_ge(s_lsig, g + 1)
                nc.scalar.activation(decay[:, :], lsig[:, :], ACT.Exp, scale=1.0 / NORMALIZER).then_inc(s_decay, 1)
                act.wait_ge(s_dq, g + 1)
                nc.scalar.activation(e_q[:, :], dq[:, :], ACT.Exp, scale=1.0 / NORMALIZER).then_inc(s_eq, 1)
                nc.scalar.activation(e_k[:, :], dq[:, :], ACT.Exp, scale=-1.0 / NORMALIZER).then_inc(s_ek, 1)
                act.wait_ge(s_drc, g + 1)
                act.wait_ge(s_kc, TPG * g)
                nc.scalar.activation(e_r[:, :], drc[:, :], ACT.Exp, scale=1.0 / NORMALIZER).then_inc(s_er, 1)

            def a_aug(g):
                act.wait_ge(s_z, g + 1)
                act.wait_ge(s_o, g)
                nc.scalar.activation(tz[:, :], z[:, :], ACT.Tanh, scale=0.5).then_inc(s_tz, 1)

            def a_square(g):
                act.wait_ge(s_dev, g + 1)
                act.wait_ge(s_oss, g)
                nc.scalar.activation(sq1[:, :], dev[:, :], ACT.Square).then_inc(s_sq1, 1)

            def a_values(g):
                act.wait_ge(s_VX, g + 1)
                act.wait_ge(s_PV, 2 * TPG * g)
                for half in range(2):
                    rows = slice(L * half, L * half + L)
                    dst = v_x[rows, :].rearrange("p (b q u v) -> p b q u v", b=SEQ, q=PAIRS, u=2)[:, :, :, half, 0:XD]
                    src = S[rows, :].rearrange("p (b q u v) -> p b q u v", b=SEQ, q=PAIRS, u=2)[:, :, :, half, :]
                    last = nc.scalar.copy(dst, src)
                last.then_inc(s_vx, 1)

            def b_queries(g):
                act.wait_ge(s_T2, g + 1)
                nc.scalar.copy(xT2[:, :], PT[:, :]).then_inc(s_xT2, 1)

            def b_queries2(g):
                act.wait_ge(s_Q, g + 1)
                act.wait_ge(s_S, TPG * g)
                nc.scalar.activation(qT[:, :], PB[:, :], ACT.Copy, scale=float(XD) ** -0.5).then_inc(s_qT, 1)

            def b_exp(g, i):
                act.wait_ge(s_fold, TPG * g + i + 1)
                nc.scalar.activation(pr_v[:, i % 2, :], S[:, :], ACT.Exp).then_inc(s_exp, 1)

            def b_probs(g, i):
                act.wait_ge(s_PT, 2 * (TPG * g + i) + 2)
                act.wait_ge(s_PV, 2 * (TPG * g + i))
                nc.scalar.copy(prT[:, 512:1024], PT[:, :]).then_inc(s_prT, 1)

            def b_out(g):
                act.wait_ge(s_CX, g + 1)
                nc.scalar.copy(cxT[:, :], PT[:, :]).then_inc(s_cxT, 1)

            def b_ffn(g):
                act.wait_ge(s_T3, g + 1)
                nc.scalar.copy(xT3[:, :], PT[:, :]).then_inc(s_xT3, 1)

            def b_gelu(g):
                act.wait_ge(s_FF, g + 1)
                act.wait_ge(s_gl, g)
                nc.scalar.activation(yh[:, :], PB[:, :], ACT.Copy, scale=0.5).then_inc(s_yh, 1)
                act.wait_ge(s_yh, g + 1)
                nc.scalar.activation(ysq[:, :], yh[:, :], ACT.Square).then_inc(s_ysq, 1)

            def b_gelu2(g):
                act.wait_ge(s_yv, g + 1)
                nc.scalar.activation(yt[:, :], yv[:, :], ACT.Tanh).then_inc(s_yt, 1)

            act.wait_ge(consts, 9)
            act.wait_ge(derived, 1)

            def step(n):
                a, b, c = n + 2, n + 1, n - 1
                A, B_, N, C = has(a), has(b), has(n), has(c)
                if A:
                    a_features(a)
                if N:
                    b_exp(n, 0)
                if C:
                    b_ffn(c)
                if B_:
                    a_square(b)
                if N:
                    b_exp(n, 1)
                if B_:
                    a_context(b)
                if A:
                    a_silu(a)
                if C:
                    b_gelu(c)
                if B_:
                    a_keys(b)
                if C:
                    b_gelu2(c)
                if N:
                    b_probs(n, 0)
                    b_exp(n, 2)
                if A:
                    a_proj(a)
                    a_log(a)
                if N:
                    b_probs(n, 1)
                    b_exp(n, 3)
                if A:
                    a_decays(a)
                if N:
                    b_probs(n, 2)
                if A:
                    a_gate(a)
                if N:
                    b_probs(n, 3)
                if A:
                    a_aug(a)
                if B_:
                    a_values(b)
                if N:
                    b_out(n)
                if B_:
                    b_queries(b)
                    b_queries2(b)

            steps(act, step)

        @block.vector
        def _(dve):
            def stats(g, n, src, st, mv, s_st, s_mv, s_xn):
                dve.wait_ge(s_xn, g)
                stv = cut(st, TPG, 6)
                for i in range(TPG):
                    last = nc.vector.bn_stats(stv[:, i, :], src(i))
                last.then_inc(s_st, 1)
                dve.wait_ge(s_st, g + 1)
                bear(n)
                for i in range(TPG):
                    last = nc.vector.bn_aggr(mv[:, 2 * i:2 * i + 2], stv[:, i, :])
                last.then_inc(s_mv, 1)

            def a_stats(g):
                stats(g, 0, lambda i: x_all[:, bass.ds((TPG * g + i) * E, E)], st1, mv1, s_st1, s_mv1, s_xn1)

            def norm(g, s_rs, s_read, s_xn, mv, rs, dst):
                dve.wait_ge(s_rs, g + 1)
                dve.wait_ge(s_read, g)
                for i in range(TPG):
                    last = nc.vector.tensor_scalar(dst[:, E * i:E * i + E], x_all[:, bass.ds((TPG * g + i) * E, E)],
                                                   mv[:, 2 * i:2 * i + 1], rs[:, i:i + 1],
                                                   ALU.subtract, ALU.mult)
                last.then_inc(s_xn, 1)

            def a_norm(g):
                norm(g, s_rs1, s_xT, s_xn1, mv1, rs1, xn1)

            def b_norm2(g):
                norm(g, s_rs2, s_T2, s_xn2, mv2, rs2, xn2)

            def a_conv(g):
                yv_ = cut(y, SEQ, L)
                dve.wait_ge(s_xpad, g + 1)
                nc.vector.tensor_scalar(yv_, xpad_v[:, :, 0:L], conv_half[:, 0:1], None, ALU.mult).then_inc(s_conv, 1)
                for k in range(1, TAPS):
                    dve.wait_ge(s_conv, TAPS * g + k)
                    nc.vector.scalar_tensor_tensor(out=yv_, in0=xpad_v[:, :, k:k + L], scalar=conv_half[:, k:k + 1],
                                                   in1=yv_, op0=ALU.mult, op1=ALU.add).then_inc(s_conv, 1)

            def a_silu(g):
                dve.wait_ge(s_th1, g + 1)
                dve.wait_ge(s_Gt, g)
                nc.vector.scalar_tensor_tensor(out=xcT[:, :], in0=th1[:, :], scalar=1.0, in1=y[:, :],
                                               op0=ALU.add, op1=ALU.mult).then_inc(s_xc, 1)

            def a_gate(g):
                dve.wait_ge(s_tg, g + 1)
                dve.wait_ge(s_og, g)
                nc.vector.scalar_tensor_tensor(out=sg[:, :], in0=tg[:, :], scalar=1.0, in1=gh[:, :],
                                               op0=ALU.add, op1=ALU.mult).then_inc(s_sg, 1)

            def a_decays(g):
                dve.wait_ge(s_ln, g + 1)
                dve.wait_ge(s_decay, g)
                nc.vector.scalar_tensor_tensor(out=lsig[:, :], in0=kg_s, scalar=0.0, in1=ln1p[:, :],
                                               op0=ALU.min, op1=ALU.subtract).then_inc(s_lsig, 1)
                dve.wait_ge(s_lsig, g + 1)
                nc.vector.tensor_scalar(lclip[:, :], lsig[:, :], LEAST_LOG, None, ALU.max).then_inc(s_lclip, 1)
                dve.wait_ge(s_lclip, g + 1)
                nc.vector.tensor_tensor_scan(G[:, :], carry[:, :], lclip[:, :], 0.0, ALU.mult, ALU.add).then_inc(s_G, 1)
                dve.wait_ge(s_G, g + 1)
                Gv = cut(G, TPG * NCH, CH)
                ref = cut(G, TPG, NCH, CH)[:, :, :, REF]
                dve.wait_ge(s_ek, g)
                nc.vector.tensor_tensor(cut(dq, TPG * NCH, CH), Gv,
                                        Gv[:, :, REF:REF + 1].to_broadcast([P, TPG * NCH, CH]),
                                        ALU.subtract).then_inc(s_dq, 1)
                nc.vector.tensor_tensor(cut(dr, TPG, NCH, NCH), ref.unsqueeze(3).to_broadcast([P, TPG, NCH, NCH]),
                                        ref.unsqueeze(2).to_broadcast([P, TPG, NCH, NCH]),
                                        ALU.subtract).then_inc(s_dr, 1)
                dve.wait_ge(s_dr, g + 1)
                dve.wait_ge(s_er, g)
                nc.vector.tensor_scalar(drc[:, :], dr[:, :], 0.0, None, ALU.min).then_inc(s_drc, 1)

            def a_keys(g):
                dve.wait_ge(s_decay, g + 1)
                nc.vector.tensor_scalar(key[:, :], decay[:, :], -1.0, 1.0, ALU.mult, ALU.add).then_inc(s_key, 1)
                dve.wait_ge(s_key, g + 1)
                dve.wait_ge(s_AUG, g)
                nc.vector.tensor_tensor(qkp[:, :], q_s, key[:, :], ALU.mult).then_inc(s_qkp, 1)
                dve.wait_ge(s_eq, g + 1)
                dve.wait_ge(s_qbd, 16 * NB * g)
                nc.vector.scalar_tensor_tensor(out=qs[:, :], in0=q_s, scalar=float(DKH) ** -0.5, in1=e_q[:, :],
                                               op0=ALU.mult, op1=ALU.mult).then_inc(s_qs, 1)
                dve.wait_ge(s_ek, g + 1)
                dve.wait_ge(s_kc, TPG * g)
                nc.vector.tensor_tensor(ke[:, :], key[:, :], e_k[:, :], ALU.mult).then_inc(s_ke, 1)

            def a_mask(g, j):
                dve.wait_ge(s_AT, 2 * g + j + 1)
                dve.wait_ge(s_AV, 2 * g)
                bear(3 + j)
                mask = cut(causal, NCH, CH).unsqueeze(2).to_broadcast([P, NCH, NB, CH])
                nc.vector.copy_predicated(at_c[:, j, :, :, :], mask, cut(AT, NCH, NB, CH)).then_inc(s_at, 1)

            def a_aug(g):
                dve.wait_ge(s_AUG, g + 1)
                dve.wait_ge(s_vt, g + 1)
                dve.wait_ge(s_tz, g)
                nc.vector.tensor_tensor(cut(z, TPG * H, DVH),
                                        PA0[:, 0:TPG * H].unsqueeze(2).to_broadcast([P, TPG * H, DVH]),
                                        cut(vt, TPG * H, DVH), ALU.mult).then_inc(s_z, 1)

            def a_center(g):
                dve.wait_ge(s_tz, g + 1)
                dve.wait_ge(s_AV, 2 * g + 2)
                nc.vector.scalar_tensor_tensor(out=o_s[:, :], in0=tz[:, :], scalar=0.5, in1=PA1[:, :],
                                               op0=ALU.mult, op1=ALU.add).then_inc(s_o, 1)
                dve.wait_ge(s_o, g + 1)
                nc.vector.tensor_reduce(osum[:, :], cut(o_s, TPG * H, DVH), AX.X, ALU.add).then_inc(s_osum, 1)
                dve.wait_ge(s_osum, g + 1)
                nc.vector.tensor_scalar(omean[:, :], osum[:, :], 1.0 / DVH, None, ALU.mult).then_inc(s_omean, 1)
                dve.wait_ge(s_omean, g + 1)
                dve.wait_ge(s_on, g)
                nc.vector.tensor_tensor(cut(dev, TPG * H, DVH), cut(o_s, TPG * H, DVH),
                                        omean[:, :].unsqueeze(2).to_broadcast([P, TPG * H, DVH]),
                                        ALU.subtract).then_inc(s_dev, 1)

            def a_squares(g):
                dve.wait_ge(s_sq1, g + 1)
                nc.vector.tensor_reduce(oss[:, :], cut(sq1, TPG * H, DVH), AX.X, ALU.add).then_inc(s_oss, 1)
                dve.wait_ge(s_oss, g + 1)
                dve.wait_ge(s_ors, g)
                nc.vector.tensor_scalar(ove[:, :], oss[:, :], 1.0 / DVH, EPS, ALU.mult, ALU.add).then_inc(s_ove, 1)

            def a_gated(g):
                dve.wait_ge(s_OT, g + 1)
                dve.wait_ge(s_sg, g + 1)
                dve.wait_ge(s_Y, g)
                nc.vector.tensor_tensor(ogT[:, :], PA0[:, :], sg[:, :], ALU.mult).then_inc(s_og, 1)

            def a_residual(g):
                dve.wait_ge(s_Y, g + 1)
                at_g = x_all[:, bass.ds(g * GT, GT)]
                nc.vector.tensor_tensor(at_g, PA1[:, :], at_g, ALU.add).then_inc(s_x1, 1)

            def b_stats2(g):
                dve.wait_ge(s_x1, g + 1)
                stats(g, 1, lambda i: x_all[:, bass.ds((TPG * g + i) * E, E)], st2, mv2, s_st2, s_mv2, s_xn2)

            def b_max(g, i):
                dve.wait_ge(s_S, TPG * g + i + 1)
                dve.wait_ge(s_fold, TPG * g + i)
                nc.vector.tensor_reduce(nmax[:, :], cut(S, XH, L), AX.X, ALU.max, negate=True).then_inc(s_max, 1)

            def b_probs(g, i):
                dve.wait_ge(s_PT, 2 * (TPG * g + i) + 1)
                if not isinstance(g, int) or TPG * g + i > 0:
                    dve.wait_ge(s_PV, 2 * (TPG * g + i) - 1)
                nc.vector.tensor_copy(prT[:, 0:512], PT[:, :]).then_inc(s_prT, 1)

            def b_weigh(g, i):
                dve.wait_ge(s_PV, 2 * (TPG * g + i) + 2)
                pv = PB[:, 0:XH * VC].rearrange("p (h v) -> p h v", h=XH)
                nc.vector.reciprocal(rden[:, :].unsqueeze(2), pv[:, :, XD:VC]).then_inc(s_rden, 1)
                dve.wait_ge(s_rden, TPG * g + i + 1)
                if i == 0:
                    dve.wait_ge(s_CX, g)
                nc.vector.tensor_tensor(cx[:, E * i:E * i + E].rearrange("p (h v) -> p h v", h=XH), pv[:, :, 0:XD],
                                        rden[:, :].unsqueeze(2).to_broadcast([P, XH, XD]),
                                        ALU.mult).then_inc(s_cx, 1)

            def b_residual(g):
                dve.wait_ge(s_WO, g + 1)
                dve.wait_ge(s_yout, g)
                nc.vector.tensor_tensor(x2[:, :], PB[:, :], x_all[:, bass.ds(g * GT, GT)], ALU.add).then_inc(s_x2, 1)
                dve.wait_ge(s_x2, g + 1)
                stats(g, 2, lambda i: x2[:, E * i:E * i + E], st3, mv3, s_st3, s_mv3, s_xn3)

            def b_route(g):
                dve.wait_ge(s_RT, g + 1)
                nc.vector.tensor_copy(rs_all[:, :], PT[:, 0:KH]).then_inc(s_rall, 1)

            def b_route2(g):
                dve.wait_ge(s_rall, g + 1)
                alls = cut(rs_all, TPG, L)
                nc.vector.tensor_tensor(cut(own, TPG, L), alls, same[:, :].unsqueeze(1).to_broadcast([P, TPG, L]),
                                        ALU.mult).then_inc(s_own, 1)
                dve.wait_ge(s_own, g + 1)
                nc.vector.tensor_reduce(r_own[:, :], cut(own, TPG, L), AX.X, ALU.add).then_inc(s_rown, 1)
                dve.wait_ge(s_rown, g + 1)
                mine = r_own[:, :].unsqueeze(2).to_broadcast([P, TPG, L])
                nc.vector.tensor_tensor(cut(above, TPG, L), alls, mine, ALU.is_gt).then_inc(s_above, 1)
                nc.vector.tensor_tensor(cut(tied, TPG, L), alls, mine, ALU.is_equal).then_inc(s_tied, 1)
                dve.wait_ge(s_tied, g + 1)
                nc.vector.tensor_tensor(cut(tiedb, TPG, L), cut(tied, TPG, L),
                                        before[:, :].unsqueeze(1).to_broadcast([P, TPG, L]),
                                        ALU.mult).then_inc(s_tiedb, 1)
                dve.wait_ge(s_tiedb, g + 1)
                nc.vector.tensor_tensor(cnt[:, :], above[:, :], tiedb[:, :], ALU.add).then_inc(s_cnt, 1)
                dve.wait_ge(s_cnt, g + 1)
                nc.vector.tensor_reduce(rank[:, :], cut(cnt, TPG, L), AX.X, ALU.add).then_inc(s_rank, 1)
                dve.wait_ge(s_rank, g + 1)
                nc.vector.tensor_scalar(taken[:, :], rank[:, :], float(KEEP), None, ALU.is_lt).then_inc(s_taken, 1)

            def b_gelu(g):
                dve.wait_ge(s_ysq, g + 1)
                nc.vector.tensor_scalar(yu[:, :], ysq[:, :], 8.0 * GELU_A * GELU_C, 2.0 * GELU_C, ALU.mult,
                                        ALU.add).then_inc(s_yu, 1)
                dve.wait_ge(s_yu, g + 1)
                nc.vector.tensor_tensor(yv[:, :], yu[:, :], yh[:, :], ALU.mult).then_inc(s_yv, 1)

            def b_result(g, part):
                if part == 0:
                    dve.wait_ge(s_yt, g + 1)
                    nc.vector.scalar_tensor_tensor(out=gl[:, :], in0=yt[:, :], scalar=1.0, in1=yh[:, :],
                                                   op0=ALU.add, op1=ALU.mult).then_inc(s_gl, 1)
                    return
                dve.wait_ge(s_gl, g + 1)
                dve.wait_ge(s_taken, g + 1)
                dve.wait_ge(s_xn3, g + 1)
                bear(5)
                take = taken[:, :].bitcast(u32).unsqueeze(2).to_broadcast([P, TPG, E])
                nc.vector.copy_predicated(cut(xn3, TPG, E), take, cut(gl, TPG, E)).then_inc(s_sel, 1)
                dve.wait_ge(s_sel, g + 1)
                dve.wait_ge(s_out, 16 * g)
                nc.vector.tensor_tensor(yout[:, :], xn3[:, :], x2[:, :], ALU.add).then_inc(s_yout, 1)

            nc.vector.memset(bearer[:, :], 0.0).then_inc(clear, 1)
            dve.wait_ge(clear, 1)
            dve.wait_ge(x_in, 16)
            a_stats(0)
            a_norm(0)
            nc.vector.memset(k_bd[:, :], 0.0).then_inc(clear, 1)
            nc.vector.memset(v_bd[:, :], 0.0)
            nc.vector.memset(at[:, :], 0.0)
            nc.vector.memset(v_x[:, :], 0.0).then_inc(clear, 1)
            dve.wait_ge(clear, 3)
            for half in range(2):
                ones = v_x[L * half:L * half + L, :].rearrange("p (b q u v) -> p b q u v", b=SEQ, q=PAIRS, u=2)
                nc.vector.memset(ones[:, :, :, half, XD:VC].rearrange("p b q v -> p (b q) v"), 1.0)
            dve.wait_ge(w_in, W_IN)
            dve.wait_ge(consts2, 10)
            nc.vector.tensor_copy(ident_b[:, :], ident[:, :])
            nc.vector.tensor_copy(causal[:, :], causal_f[:, :])
            nc.vector.tensor_scalar(conv_half[:, :], conv_s[:, :], 0.5, None, ALU.mult)
            nc.vector.tensor_scalar(bg_half[:, :], bg_s[:, :], 0.5, None, ALU.mult)
            nc.vector.tensor_scalar(aug_sel[:, :], block_of[:, :], aug_s[:, 0:1], None, ALU.mult)
            nc.vector.tensor_copy(wr_rep[:, :], wr_s[:, 0:1].to_broadcast([P, L])).then_inc(derived, 1)
            dve.wait_ge(derived, 1)
            dve.wait_ge(x_rest, 16)

            def step(n):
                a, b, c = n + 2, n + 1, n - 1
                A, B_, N, C = has(a), has(b), has(n), has(c)
                if N:
                    b_max(n, 0)
                if B_:
                    a_center(b)
                if A:
                    a_conv(a)
                if N:
                    b_max(n, 1)
                if C:
                    b_route(c)
                if N:
                    b_probs(n, 0)
                if B_:
                    a_squares(b)
                if A:
                    a_silu(a)
                if C:
                    b_gelu(c)
                if N:
                    b_max(n, 2)
                    b_probs(n, 1)
                    b_weigh(n, 0)
                if C:
                    b_result(c, 0)
                    b_route2(c)
                if A:
                    a_decays(a)
                if N:
                    b_max(n, 3)
                if A:
                    a_keys(a)
                if N:
                    b_probs(n, 2)
                    b_weigh(n, 1)
                if B_:
                    a_gated(b)
                if C:
                    b_result(c, 1)
                if B_:
                    a_residual(b)
                    b_stats2(b)
                if N:
                    b_probs(n, 3)
                    b_weigh(n, 2)
                if A:
                    a_gate(a)
                    a_aug(a)
                if B_:
                    b_norm2(b)
                if A:
                    a_mask(a, 0)
                if N:
                    b_weigh(n, 3)
                if A:
                    a_mask(a, 1)
                if has(a + 1):
                    a_stats(a + 1)
                if N:
                    b_residual(n)
                if has(a + 1):
                    a_norm(a + 1)

            steps(dve, step)


_SHAPE = (64, 64, 128)


def kernel(x, ctx_1024, mask_1_bf0, L0_attn_conv_w, L0_attn_wq, L0_attn_wkg, L0_attn_wv, L0_attn_wg, L0_attn_bg,
           L0_attn_wout, L0_attn_aug_balance, L0_xattn_Wq, L0_xattn_Wk, L0_xattn_Wv, L0_xattn_Wo,
           L0_ffn_w_router, L0_ffn_w_block):
    import numpy as np
    import concourse.bacc as bacc
    from concourse.bass_utils import run_bass_kernel_spmd

    ins = {
        "x": x, "ctx": ctx_1024, "conv_w": L0_attn_conv_w, "wq": L0_attn_wq, "wkg": L0_attn_wkg,
        "wv": L0_attn_wv, "wg": L0_attn_wg, "bg": np.asarray(L0_attn_bg)[:, None], "wout": L0_attn_wout,
        "aug": np.asarray(L0_attn_aug_balance)[:, None], "WqT": np.asarray(L0_xattn_Wq).T,
        "WkT": np.asarray(L0_xattn_Wk).T, "WvT": np.asarray(L0_xattn_Wv).T, "WoT": np.asarray(L0_xattn_Wo).T,
        "w_router": np.asarray(L0_ffn_w_router)[:, None], "w_block": L0_ffn_w_block,
    }
    nc = bacc.Bacc("TRN2", target_bir_lowering=False, num_devices=1)
    arrays, args = {}, []
    for name, a in ins.items():
        a = np.ascontiguousarray(a)
        arrays[f"in_{name}"] = a
        args.append(nc.dram_tensor(f"in_{name}", a.shape, mybir.dt.from_np(a.dtype), kind="ExternalInput").ap())
    args.append(nc.dram_tensor("out_0", _SHAPE, mybir.dt.float32, kind="ExternalOutput").ap())
    decoder_layer(nc, *args)
    r = run_bass_kernel_spmd(nc, [arrays], core_ids=[0])
    return r.results[0]["out_0"]
```

```python
import concourse.bass as bass
from concourse import mybir
from contextlib import ExitStack


def decoder_layer(
    nc: bass.Bass,
    x: bass.AP, ctx_in: bass.AP, conv_w: bass.AP, wq: bass.AP, wkg: bass.AP, wv: bass.AP, wg: bass.AP,
    bg: bass.AP, wout: bass.AP, aug: bass.AP, WqT: bass.AP, WkT: bass.AP, WvT: bass.AP, WoT: bass.AP,
    w_router: bass.AP, w_block: bass.AP, out: bass.AP,
):
    fp32 = mybir.dt.float32
    bf16 = mybir.dt.bfloat16
    u32 = mybir.dt.uint32
    ALU = mybir.AluOpType
    ACT = mybir.ActivationFunctionType
    AX = mybir.AxisListType

    B, L, E = x.shape
    P = 128
    TPG = 4
    NT = B * L // P
    NG = NT // TPG
    GT = TPG * P
    SEQ = GT // L
    DK = wq.shape[1]
    H = 8
    DKH, DVH = DK // H, E // H
    XH = 16
    XD = E // XH
    NB = 2 * H
    KH = TPG * L
    TAPS = conv_w.shape[1]
    PADL = TAPS - 1 + L
    CH = 8
    NCH = L // CH
    REF = CH // 2 - 1
    NORMALIZER = 16.0
    LEAST_LOG = -20.0 * NORMALIZER
    EPS = 1e-5
    KEEP = max(1, int(L * 0.75))
    GELU_C, GELU_A = 0.7978845608028654, 0.044715
    PAIRS = XH // 2
    VC = XD + 1
    RUN = 64
    RUNS = P // RUN
    XHG = XH // RUNS

    x_tiles = x.rearrange("b l e -> (b l) e").rearrange("(t p) e -> p t e", p=P)
    ctx_tiles = ctx_in.rearrange("b l e -> (b l) e").rearrange("(t p) e -> p t e", p=P)
    out_tiles = out.rearrange("b l e -> (b l) e").rearrange("(t p) e -> p t e", p=P)

    stack = ExitStack()
    with stack:
        def sb(name, cols, dt=fp32, parts=P):
            return stack.enter_context(nc.sbuf_tensor(name, [parts, cols], dt))

        def sem(name):
            return stack.enter_context(nc.semaphore(name))

        def cut(t, *dims):
            a = t[:, :]
            names = "abcd"[:len(dims)]
            return a.rearrange(f"p ({' '.join(names)}) -> p {' '.join(names)}",
                               **{n: d for n, d in zip(names, dims)})

        ident = sb("ident", P)
        ident_b = sb("ident_b", P, bf16)
        causal = sb("causal", L, u32)
        causal_f = sb("causal_f", L)
        before = sb("before", L)
        same = sb("same", L)
        block_of = sb("block_of", NB)
        head_of = sb("head_of", XHG)
        aug_sel = sb("aug_sel", NB)
        carry = sb("carry", KH)
        minus_half = sb("minus_half", TPG * H)
        eps_s = sb("eps_s", TPG)
        bearer = sb("bearer", 7)
        wq_s, wkg_s = sb("wq_s", DK), sb("wkg_s", DK)
        wv_s, wg_s, wout_s = sb("wv_s", E), sb("wg_s", E), sb("wout_s", E)
        WqT_s, WkT_s, WvT_s, WoT_s = sb("WqT_s", E), sb("WkT_s", E), sb("WvT_s", E), sb("WoT_s", E)
        wblk_s = sb("wblk_s", E)
        wr_s = sb("wr_s", 1)
        wr_rep = sb("wr_rep", L)
        conv_s, bg_s, aug_s = sb("conv_s", TAPS), sb("bg_s", 1), sb("aug_s", 1)
        conv_half, bg_half = sb("conv_half", TAPS), sb("bg_half", 1)

        x_all = sb("x_all", NT * E)
        xa = cut(x_all, NT, E)
        st1, mv1, ve1, rs1 = sb("st1", TPG * 6), sb("mv1", TPG * 2), sb("ve1", TPG), sb("rs1", TPG)
        xn1 = sb("xn1", GT)
        xpad = sb("xpad", SEQ * PADL)
        xpad_v = cut(xpad, SEQ, PADL)
        y = sb("y", GT)
        th1 = sb("th1", GT)
        xcT = sb("xcT", GT)
        qk = sb("qk", 2 * KH)
        q_s, kg_s = qk[:, 0:KH], qk[:, KH:2 * KH]
        ab, ex, ln1p, lsig = sb("ab", KH), sb("ex", KH), sb("ln1p", KH), sb("lsig", KH)
        decay, key, lclip, G = sb("decay", KH), sb("key", KH), sb("lclip", KH), sb("G", KH)
        dq, dr = sb("dq", KH), sb("dr", TPG * NCH * NCH)
        drc = sb("drc", TPG * NCH * NCH)
        e_q, e_k, e_r = sb("e_q", KH), sb("e_k", KH), sb("e_r", TPG * NCH * NCH)
        qs, ke, qkp = sb("qs", KH), sb("ke", KH), sb("qkp", KH)
        kc = sb("kc", TPG * NCH * L)
        kc_m = cut(kc, TPG, NCH, L)
        q_bd = sb("q_bd", NB * KH)
        q_bdv = cut(q_bd, NB, KH)
        vt = sb("vt", GT)
        v_bd = sb("v_bd", 2 * 2 * 2 * E)
        v_bdv = v_bd[:, :].rearrange("p (j x w f) -> p j x w f", j=2, x=2, w=2)
        at = sb("at", 2 * NB * L)
        at_m = cut(at, 2, NB, L)
        at_c = at[:, :].rearrange("p (j n c s) -> p j c n s", j=2, n=NB, c=NCH)
        gh, tg, sg = sb("gh", GT), sb("tg", GT), sb("sg", GT)
        z, tz, o_s, dev, sq1, on = (sb(n, GT) for n in ("z", "tz", "o_s", "dev", "sq1", "on"))
        osum, omean, oss, ove, ors = (sb(n, TPG * H) for n in ("osum", "omean", "oss", "ove", "ors"))
        ogT = sb("ogT", GT)
        c_s, cT = sb("c_s", GT), sb("cT", GT)
        kx = sb("kx", GT)
        k_bd = sb("k_bd", XHG * GT)
        k_bdv = cut(k_bd, XHG, GT)
        v_x = sb("v_x", SEQ * PAIRS * 2 * VC)
        v_xv = cut(v_x, SEQ, PAIRS, 2 * VC)

        st2, mv2, ve2, rs2 = sb("st2", TPG * 6), sb("mv2", TPG * 2), sb("ve2", TPG), sb("rs2", TPG)
        xn2, xT2 = sb("xn2", GT), sb("xT2", GT)
        qT = sb("qT", RUNS * GT)
        qT_v = cut(qT, RUNS, GT)
        nmax = sb("nmax", XH, bf16)
        pr = sb("pr", 2 * XH * L)
        pr_v = cut(pr, 2, XH * L)
        prT = sb("prT", PAIRS * P)
        prT_v = cut(prT, PAIRS, P)
        rden = sb("rden", XH)
        cx, cxT, x2 = sb("cx", GT), sb("cxT", GT), sb("x2", GT)
        st3, mv3, ve3, rs3 = sb("st3", TPG * 6), sb("mv3", TPG * 2), sb("ve3", TPG), sb("rs3", TPG)
        xn3, xT3 = sb("xn3", GT), sb("xT3", GT)
        yh, ysq, yu, yv, yt, gl = (sb(n, GT) for n in ("yh", "ysq", "yu", "yv", "yt", "gl"))
        rs_all = sb("rs_all", KH)
        own, r_own = sb("own", KH), sb("r_own", TPG)
        above, tied, tiedb, cnt = sb("above", KH), sb("tied", KH), sb("tiedb", KH), sb("cnt", KH)
        rank, taken = sb("rank", TPG), sb("taken", TPG)
        yout = sb("yout", GT)

        def ps(name, cols):
            return stack.enter_context(nc.psum_tensor(name, [P, cols], fp32))

        PA0, PA1, AT = ps("PA0", 512), ps("PA1", 512), ps("AT", 1024)
        S, PT, PB = ps("S", 1024), ps("PT", 512), ps("PB", 512)
        AT0, AT1 = AT[:, 0:512], AT[:, 512:1024]

        w_in, w_later, x_in, x_rest, c_in = (sem(n) for n in ("w_in", "w_later", "x_in", "x_rest", "c_in"))
        consts, consts2, derived = sem("consts"), sem("consts2"), sem("derived")
        q_clear, borne, zeros = sem("q_clear"), sem("borne"), sem("zeros")
        s_st1, s_mv1, s_ve1, s_rs1, s_xn1 = (sem(n) for n in ("s_st1", "s_mv1", "s_ve1", "s_rs1", "s_xn1"))
        s_xT, s_xpad, s_conv, s_th1, s_xc = (sem(n) for n in ("s_xT", "s_xpad", "s_conv", "s_th1", "s_xc"))
        s_QK, s_V, s_Gt, s_qk, s_vt = (sem(n) for n in ("s_QK", "s_V", "s_Gt", "s_qk", "s_vt"))
        s_ab, s_ex, s_ln, s_lsig, s_decay, s_key = (
            sem(n) for n in ("s_ab", "s_ex", "s_ln", "s_lsig", "s_decay", "s_key"))
        s_lclip, s_G, s_dq, s_dr, s_drc = (sem(n) for n in ("s_lclip", "s_G", "s_dq", "s_dr", "s_drc"))
        s_eq, s_ek, s_er, s_qs, s_ke, s_qkp, s_kc = (
            sem(n) for n in ("s_eq", "s_ek", "s_er", "s_qs", "s_ke", "s_qkp", "s_kc"))
        s_qbd, s_vbd = sem("s_qbd"), sem("s_vbd")
        s_AUG, s_AT, s_at, s_AV = (sem(n) for n in ("s_AUG", "s_AT", "s_at", "s_AV"))
        s_gh, s_tg, s_sg = (sem(n) for n in ("s_gh", "s_tg", "s_sg"))
        s_z, s_tz, s_o, s_osum, s_omean, s_dev, s_sq1, s_oss = (
            sem(n) for n in ("s_z", "s_tz", "s_o", "s_osum", "s_omean", "s_dev", "s_sq1", "s_oss"))
        s_ove, s_ors, s_on, s_OT, s_og, s_Y, s_x1 = (
            sem(n) for n in ("s_ove", "s_ors", "s_on", "s_OT", "s_og", "s_Y", "s_x1"))
        s_CT, s_cT, s_KX, s_kx, s_VX, s_vx = (sem(n) for n in ("s_CT", "s_cT", "s_KX", "s_kx", "s_VX", "s_vx"))
        s_kbd, s_kbd2 = sem("s_kbd"), sem("s_kbd2")
        s_st2, s_mv2, s_ve2, s_rs2, s_xn2 = (sem(n) for n in ("s_st2", "s_mv2", "s_ve2", "s_rs2", "s_xn2"))
        s_T2, s_xT2, s_Q, s_qT = (sem(n) for n in ("s_T2", "s_xT2", "s_Q", "s_qT"))
        s_S, s_max, s_fold, s_exp = (sem(n) for n in ("s_S", "s_max", "s_fold", "s_exp"))
        s_PT, s_prT = sem("s_PT"), sem("s_prT")
        s_PV = sem("s_PV")
        s_rden, s_cx = sem("s_rden"), sem("s_cx")
        s_CX, s_cxT, s_WO, s_x2 = (sem(n) for n in ("s_CX", "s_cxT", "s_WO", "s_x2"))
        s_st3, s_mv3, s_ve3, s_rs3, s_xd3, s_xn3 = (
            sem(n) for n in ("s_st3", "s_mv3", "s_ve3", "s_rs3", "s_xd3", "s_xn3"))
        s_T3, s_xT3, s_FF, s_RT = (sem(n) for n in ("s_T3", "s_xT3", "s_FF", "s_RT"))
        s_yh, s_ysq, s_yu, s_yv, s_yt, s_gl = (sem(n) for n in ("s_yh", "s_ysq", "s_yu", "s_yv", "s_yt", "s_gl"))
        s_rall, s_own, s_rown, s_above, s_tied, s_tiedb, s_cnt, s_rank, s_taken = (
            sem(n) for n in ("s_rall", "s_own", "s_rown", "s_above", "s_tied", "s_tiedb", "s_cnt", "s_rank",
                             "s_taken"))
        s_sel, s_yout, s_out = sem("s_sel"), sem("s_yout"), sem("s_out")

        WEIGHTS = [(conv_s[:, :], conv_w), (wq_s[:, :], wq), (wkg_s[:, :], wkg), (wv_s[:, :], wv), (wg_s[:, :], wg),
                   (wr_s[:, :], w_router), (bg_s[:, :], bg), (aug_s[0:DK, :], aug), (aug_s[DK:2 * DK, :], aug)]
        LATER = [(wout_s[:, :], wout), (WqT_s[:, :], WqT), (WkT_s[:, :], WkT), (WvT_s[:, :], WvT),
                 (WoT_s[:, :], WoT), (wblk_s[:, :], w_block)]

        def bear(n):
            nc.vector.tensor_copy(bearer[:, 1 + n:2 + n], bearer[:, 0:1])

        def has(g):
            return not isinstance(g, int) or 0 <= g < NG

        def upto(g):
            return min(g, NG) if isinstance(g, int) else g

        FIRST, LAST = 2, NG - 3

        def steps(eng, fill, step, drain):
            for n in range(-2, 0):
                fill(n)
            for n in range(FIRST):
                step(n)
            with eng.Fori(FIRST, LAST) as n:
                step(n)
            for n in range(LAST, NG - 1):
                step(n)
            for n in range(NG - 1, NG + 1):
                drain(n)

        block = stack.enter_context(nc.Block())

        @block.sync
        def _(sp):
            def held(v):
                return v if isinstance(v, int) else sp.to_reg(v)

            def load_ctx(g):
                sp.wait_ge(s_CT, g)
                sp.dma_start(cut(c_s, TPG, E), ctx_tiles[:, bass.ds(TPG * g, TPG), :]).then_inc(c_in, 16)

            def queries_to_blocks(g):
                scaled, scored = held(g + 1), held(2 * g)
                sp.wait_ge(s_qs, scaled)
                sp.wait_ge(s_AT, scored)
                for n in range(NB):
                    sp.dma_start(q_bdv[8 * n:8 * n + 8, n, :], qs[8 * n:8 * n + 8, :]).then_inc(s_qbd, 16)

            def values_to_blocks(g):
                copied, used = held(g + 1), held(2 * g)
                sp.wait_ge(s_vt, copied)
                sp.wait_ge(s_AV, used)
                for half in range(2):
                    for w in range(2):
                        src = vt[L * half:L * half + L, :].rearrange("p (j w f) -> p j w f", j=2, w=2)[:, :, w, :]
                        sp.dma_start(v_bdv[L * w:L * w + L, :, half, w, :], src).then_inc(s_vbd, 16)

            def store(g):
                ready = held(g + 1)
                sp.wait_ge(s_yout, ready)
                sp.dma_start(out_tiles[:, bass.ds(TPG * g, TPG), :], cut(yout, TPG, E)).then_inc(s_out, 16)

            def load(weights, done):
                for dst, src in weights:
                    sp.dma_start(dst, src).then_inc(done, 16)

            sp.dma_start(xa[:, 0:TPG, :], x_tiles[:, 0:TPG, :]).then_inc(x_in, 16)
            load(WEIGHTS, w_in)
            load(LATER, w_later)
            sp.dma_start(xa[:, TPG:NT, :], x_tiles[:, TPG:NT, :]).then_inc(x_rest, 16)
            sp.wait_ge(zeros, 4)
            sp.wait_ge(q_clear, 1)

            def fill(n):
                a, b = n + 2, n + 1
                if has(a):
                    queries_to_blocks(a)
                    values_to_blocks(a)
                if has(b + 1):
                    load_ctx(b + 1)

            def step(n):
                a, b, c = n + 2, n + 1, n - 1
                if has(b + 1):
                    load_ctx(b + 1)
                if has(a):
                    queries_to_blocks(a)
                    values_to_blocks(a)
                if has(c):
                    store(c)

            def drain(n):
                c = n - 1
                if has(c):
                    store(c)







            steps(sp, fill, step, drain)
            sp.wait_ge(s_out, 16 * NG)

        @block.gpsimd
        def _(pool):
            nc.gpsimd.memset(ident[:, :], 0.0).then_inc(consts, 1)
            nc.gpsimd.memset(causal_f[:, :], 1.0).then_inc(consts, 1)
            nc.gpsimd.memset(before[:, :], 1.0).then_inc(consts, 1)
            nc.gpsimd.memset(same[:, :], 0.0).then_inc(consts, 1)
            nc.gpsimd.memset(block_of[:, :], 1.0).then_inc(consts, 1)
            nc.gpsimd.memset(carry[:, :], 1.0).then_inc(consts, 1)
            nc.gpsimd.memset(minus_half[:, :], -0.5).then_inc(consts, 1)
            nc.gpsimd.memset(xpad[:, :], 0.0).then_inc(consts, 1)
            nc.gpsimd.memset(eps_s[:, :], EPS).then_inc(consts, 1)
            pool.wait_ge(consts, 9)
            made = 0

            def select(t, keep, fill, base, step, by_row):
                nonlocal made
                nc.gpsimd.affine_select(out=t, in_=t, compare_op=keep, fill=fill, base=base,
                                        pattern=[[step, t.shape[1]]], channel_multiplier=by_row).then_inc(consts2, 1)
                made += 1
                pool.wait_ge(consts2, made)

            select(ident[:, :], ALU.not_equal, 1.0, 0, -1, 1)
            for half in range(2):
                rows = slice(L * half, L * half + L)
                select(causal_f[rows, :], ALU.is_ge, 0.0, 0, 1, -1)
                select(before[rows, :], ALU.is_gt, 0.0, 0, -1, 1)
                select(same[rows, :], ALU.not_equal, 1.0, 0, -1, 1)
            select(block_of[:, :], ALU.is_ge, 0.0, 0, -8, 1)
            select(block_of[:, :], ALU.is_ge, 0.0, 7, 8, -1)
            nc.gpsimd.memset(cut(carry, TPG, L)[:, :, 0:1], 0.0).then_inc(consts2, 1)

            def scales(g, s_mv, s_ve, s_rs, s_xn, mv, ve, rs):
                pool.wait_ge(s_mv, g + 1)
                nc.gpsimd.tensor_tensor(cut(ve, TPG, 1), cut(mv, TPG, 2)[:, :, 1:2], cut(eps_s, TPG, 1),
                                        ALU.add).then_inc(s_ve, 1)
                pool.wait_ge(s_ve, g + 1)
                pool.wait_ge(s_xn, g)
                nc.gpsimd.tensor_tensor(rs[:, :], ve[:, :], minus_half[:, 0:TPG], ALU.pow).then_inc(s_rs, 1)

            def norm(g, s_mv, s_ve, s_rs, s_xd, s_xn, s_read, src, mv, ve, rs, dst):
                scales(g, s_mv, s_ve, s_rs, s_xn, mv, ve, rs)
                for s in s_read:
                    pool.wait_ge(s, g)
                nc.gpsimd.tensor_tensor(cut(dst, TPG, E), cut(src, TPG, E),
                                        cut(mv, TPG, 2)[:, :, 0:1].to_broadcast([P, TPG, E]),
                                        ALU.subtract).then_inc(s_xd, 1)
                pool.wait_ge(s_xd, g + 1)
                pool.wait_ge(s_rs, g + 1)
                nc.gpsimd.tensor_tensor(cut(dst, TPG, E), cut(dst, TPG, E),
                                        rs[:, :].unsqueeze(2).to_broadcast([P, TPG, E]),
                                        ALU.mult).then_inc(s_xn, 1)

            def norm_a(g):
                scales(g, s_mv1, s_ve1, s_rs1, s_xn1, mv1, ve1, rs1)

            def norm_b2(g):
                scales(g, s_mv2, s_ve2, s_rs2, s_xn2, mv2, ve2, rs2)

            def norm_b3(g):
                norm(g, s_mv3, s_ve3, s_rs3, s_xd3, s_xn3, [s_T3, s_yout], x2, mv3, ve3, rs3, xn3)

            def key_blocks(g):
                pool.wait_ge(s_kx, g + 1)
                pool.wait_ge(s_S, TPG * g)
                nc.gpsimd.tensor_tensor(k_bdv[:, XHG // 2:XHG, :],
                                        kx[:, :].unsqueeze(1).to_broadcast([P, XHG // 2, GT]),
                                        head_of[:, XHG // 2:XHG].unsqueeze(2).to_broadcast([P, XHG // 2, GT]),
                                        ALU.mult).then_inc(s_kbd2, 1)

            def keys(g):
                pool.wait_ge(s_ke, g + 1)
                pool.wait_ge(s_er, g + 1)
                pool.wait_ge(s_AT, 2 * g)
                kev = cut(ke, TPG, NCH, CH)
                erv = cut(e_r, TPG, NCH, NCH)
                for i in range(TPG):
                    nc.gpsimd.tensor_tensor(
                        kc[:, i * NCH * L:(i + 1) * NCH * L].rearrange(
                            "p (c d s) -> p c d s", c=NCH, d=NCH),
                        kev[:, i, :, :].unsqueeze(1).to_broadcast([P, NCH, NCH, CH]),
                        erv[:, i, :, :].unsqueeze(3).to_broadcast([P, NCH, NCH, CH]), ALU.mult).then_inc(s_kc, 1)

            def group_norm(g):
                pool.wait_ge(s_ove, g + 1)
                nc.gpsimd.tensor_tensor(ors[:, :], ove[:, :], minus_half[:, :], ALU.pow).then_inc(s_ors, 1)
                pool.wait_ge(s_ors, g + 1)
                pool.wait_ge(s_OT, g)
                nc.gpsimd.tensor_tensor(cut(on, TPG * H, DVH), cut(dev, TPG * H, DVH),
                                        ors[:, :].unsqueeze(2).to_broadcast([P, TPG * H, DVH]),
                                        ALU.mult).then_inc(s_on, 1)

            def route(g):
                alls = cut(rs_all, TPG, L)
                pool.wait_ge(s_rall, g + 1)
                pool.wait_ge(s_rown, g)
                nc.gpsimd.tensor_tensor(cut(own, TPG, L), alls, same[:, :].unsqueeze(1).to_broadcast([P, TPG, L]),
                                        ALU.mult).then_inc(s_own, 1)

            def route2(g):
                pool.wait_ge(s_tied, g + 1)
                nc.gpsimd.tensor_tensor(cut(tiedb, TPG, L), cut(tied, TPG, L),
                                        before[:, :].unsqueeze(1).to_broadcast([P, TPG, L]),
                                        ALU.mult).then_inc(s_tiedb, 1)
                pool.wait_ge(s_tiedb, g + 1)
                pool.wait_ge(s_above, g + 1)
                pool.wait_ge(s_rank, g)
                nc.gpsimd.tensor_tensor(cnt[:, :], above[:, :], tiedb[:, :], ALU.add).then_inc(s_cnt, 1)

            def result(g):
                pool.wait_ge(s_sel, g + 1)
                pool.wait_ge(s_out, 16 * g)
                nc.gpsimd.tensor_tensor(yout[:, :], xn3[:, :], x2[:, :], ALU.add).then_inc(s_yout, 1)

            norm_a(0)
            nc.gpsimd.memset(q_bd[:, :], 0.0).then_inc(q_clear, 1)

            def fill(n):
                a, b = n + 2, n + 1
                if has(b):
                    group_norm(b)
                if has(a + 1):
                    norm_a(a + 1)
                if has(b):
                    norm_b2(b)
                if has(a):
                    keys(a)
                if has(b):
                    key_blocks(b)

            def step(n):
                a, b, c = n + 2, n + 1, n - 1
                if has(c):
                    norm_b3(c)
                    route(c)
                if has(b):
                    group_norm(b)
                if has(c):
                    route2(c)
                if has(b):
                    key_blocks(b)
                if has(a):
                    keys(a)
                if has(b):
                    norm_b2(b)
                if has(a + 1):
                    norm_a(a + 1)
                if has(c):
                    result(c)

            def drain(n):
                c = n - 1
                if has(c):
                    norm_b3(c)
                    route(c)
                    route2(c)
                    result(c)







            steps(pool, fill, step, drain)

        @block.tensor
        def _(pe):
            def to_features(dst, src):
                for i in range(TPG):
                    last = nc.tensor.transpose(dst[:, P * i:P * i + P], src[:, P * i:P * i + P], ident[:, :])
                return last

            def transpose_x(g):
                pe.wait_ge(s_xn1, g + 1)
                pe.wait_ge(s_z, g)
                to_features(PA0, xn1).then_inc(s_xT, 1)

            def transpose_ctx(g):
                pe.wait_ge(c_in, 16 * (g + 1))
                pe.wait_ge(s_o, g + 1)
                to_features(PA1, c_s).then_inc(s_CT, 1)

            def later_weights(g):
                if isinstance(g, int) and g == 0:
                    pe.wait_ge(w_later, 16 * len(LATER))

            def context_keys(g):
                later_weights(g)
                pe.wait_ge(s_cT, g + 1)
                pe.wait_ge(s_at, 2 * (g + 1))
                nc.tensor.matmul(AT1, WkT_s[:, :], cT[:, :], start=True, stop=True).then_inc(s_KX, 1)

            def context_values(g):
                later_weights(g)
                pe.wait_ge(s_cT, g + 1)
                pe.wait_ge(s_exp, TPG * g)
                for b in range(SEQ):
                    for half in range(2):
                        last = nc.tensor.matmul(S[L * half:L * half + L, E * b:E * b + E], cT[:, L * b:L * b + L],
                                                WvT_s[:, :], start=True, stop=True)
                last.then_inc(s_VX, 1)

            def project_qk(g):
                xc_h = xcT[:, :].rearrange("p (i x t) -> p i x t", i=TPG, x=2)
                pe.wait_ge(s_xc, g + 1)
                pe.wait_ge(s_xpad, g + 1)
                for n, w in enumerate((wq_s, wkg_s)):
                    for half in range(2):
                        last = nc.tensor.matmul(PA0[L * half:L * half + L, KH * n:KH * n + KH], w[:, :],
                                                xc_h[:, :, half, :], start=True, stop=True)
                last.then_inc(s_QK, 1)

            def project_v(g):
                pe.wait_ge(s_xc, g + 1)
                pe.wait_ge(s_cT, g)
                for i in range(TPG):
                    last = nc.tensor.matmul(PA1[:, E * i:E * i + E], xcT[:, P * i:P * i + P], wv_s[:, :],
                                            start=True, stop=True)
                last.then_inc(s_V, 1)

            def project_g(g):
                pe.wait_ge(s_xc, g + 1)
                pe.wait_ge(s_at, 2 * g)
                nc.tensor.matmul(AT0, wg_s[:, :], xcT[:, :], start=True, stop=True).then_inc(s_Gt, 1)

            def aug_weights(g):
                pe.wait_ge(s_qkp, g + 1)
                pe.wait_ge(s_og, g)
                for i in range(TPG):
                    for half in range(2):
                        last = nc.tensor.matmul(PA0[L * half:L * half + L, H * i:H * i + H],
                                                qkp[:, L * i:L * i + L], aug_sel[:, H * half:H * half + H],
                                                start=True, stop=True)
                last.then_inc(s_AUG, 1)

            def scores(g, j):
                pe.wait_ge(s_kc, TPG * g + 2 * j + 2)
                if j == 0:
                    pe.wait_ge(s_qbd, 16 * NB * (g + 1))
                    pe.wait_ge(s_gh, g + 1)
                    pe.wait_ge(s_kx, g)
                else:
                    pe.wait_ge(s_at, 2 * g + j)
                for c in range(NCH):
                    for w in range(2):
                        i = 2 * j + w
                        last = nc.tensor.matmul(AT[L * w:L * w + L, c * NB * CH:(c + 1) * NB * CH],
                                                kc_m[:, i, c, :],
                                                q_bdv[:, :, L * i + CH * c:L * i + CH * c + CH],
                                                start=True, stop=True)
                last.then_inc(s_AT, 1)

            def attend(g, j, part):
                heads = range(H // 2 * part, H // 2 * part + H // 2)
                pe.wait_ge(s_at, 2 * g + j + 1)
                if j == 0 and part == 0:
                    pe.wait_ge(s_vbd, 64 * (g + 1))
                    pe.wait_ge(s_x1, g)
                o_v = PA1[:, :].rearrange("p (j w f) -> p j w f", j=2, w=2)
                for h in heads:
                    for half in range(2):
                        n = H * half + h
                        last = nc.tensor.matmul(o_v[L * half:L * half + L, j, :, DVH * h:DVH * h + DVH],
                                                at_m[:, j, n, :], v_bdv[:, j, half, :, DVH * h:DVH * h + DVH],
                                                start=True, stop=True)
                if part == 1:
                    last.then_inc(s_AV, 1)

            def transpose_o(g):
                pe.wait_ge(s_on, g + 1)
                pe.wait_ge(s_qk, upto(g + 2))
                to_features(PA0, on).then_inc(s_OT, 1)

            def gla_out(g):
                later_weights(g)
                pe.wait_ge(s_og, g + 1)
                pe.wait_ge(s_vt, upto(g + 2))
                for i in range(TPG):
                    last = nc.tensor.matmul(PA1[:, E * i:E * i + E], ogT[:, P * i:P * i + P], wout_s[:, :],
                                            start=True, stop=True)
                last.then_inc(s_Y, 1)

            def queries(g):
                pe.wait_ge(s_xn2, g + 1)
                pe.wait_ge(s_cxT, g)
                to_features(PT, xn2).then_inc(s_T2, 1)

            def queries2(g):
                pe.wait_ge(s_xT2, g + 1)
                pe.wait_ge(s_x2, g)
                nc.tensor.matmul(PB[:, :], WqT_s[:, :], xT2[:, :], start=True, stop=True).then_inc(s_Q, 1)

            def x_scores(g, i):
                if i == 0:
                    pe.wait_ge(s_qT, g + 1)
                    pe.wait_ge(s_kbd, g + 1)
                    pe.wait_ge(s_kbd2, g + 1)
                    pe.wait_ge(s_vx, g + 1)
                else:
                    pe.wait_ge(s_exp, TPG * g + i)
                for r in range(RUNS):
                    for half in range(2):
                        b = 2 * i + half
                        last = nc.tensor.matmul(S[L * half:L * half + L, XHG * L * r:XHG * L * r + XHG * L],
                                                qT_v[:, r, L * b:L * b + L], k_bdv[:, :, L * b:L * b + L],
                                                start=True, stop=False, skip_group_check=True)
                last.then_inc(s_S, 1)

            def less_max(g, i):
                pe.wait_ge(s_max, TPG * g + i + 1)
                hh = XH // 2
                for n in range(2):
                    last = nc.tensor.matmul(S[:, 512 * n:512 * n + 512], ident_b[:, :],
                                            nmax[:, hh * n:hh * n + hh].unsqueeze(2).to_broadcast([P, hh, L]),
                                            start=False, stop=True, skip_group_check=True)
                last.then_inc(s_fold, 1)

            def x_attend(g, i, n):
                hp = PAIRS // 2
                if n == 0:
                    pe.wait_ge(s_exp, TPG * g + i + 1)
                pe.wait_ge(s_prT, 2 * (TPG * g + i) + n)
                if i == 0 and n == 0:
                    pe.wait_ge(s_rall, g)
                for p in range(hp):
                    last = nc.tensor.transpose(PT[:, P * p:P * p + P],
                                               pr_v[:, i % 2, P * (hp * n + p):P * (hp * n + p) + P], ident[:, :])
                last.then_inc(s_PT, 1)

            def x_values(g, i, n):
                hp = PAIRS // 2
                pe.wait_ge(s_prT, 2 * (TPG * g + i) + n + 1)
                if n == 0:
                    pe.wait_ge(s_cx, TPG * g + i)
                    if i == 0:
                        pe.wait_ge(s_yh, g)
                for p in range(hp * n, hp * n + hp):
                    for half in range(2):
                        last = nc.tensor.matmul(PB[L * half:L * half + L, 2 * VC * p:2 * VC * p + 2 * VC],
                                                prT_v[:, p, L * half:L * half + L], v_xv[:, 2 * i + half, p, :],
                                                start=True, stop=True)
                last.then_inc(s_PV, 1)

            def x_out(g):
                pe.wait_ge(s_cx, TPG * g + TPG)
                pe.wait_ge(s_prT, 2 * TPG * (g + 1))
                to_features(PT, cx).then_inc(s_CX, 1)

            def x_out2(g):
                pe.wait_ge(s_cxT, g + 1)
                for i in range(TPG):
                    last = nc.tensor.matmul(PB[:, E * i:E * i + E], cxT[:, P * i:P * i + P], WoT_s[:, :],
                                            start=True, stop=True)
                last.then_inc(s_WO, 1)

            def transpose_x2(g):
                pe.wait_ge(s_xn3, g + 1)
                pe.wait_ge(s_xT2, upto(g + 2))
                to_features(PT, xn3).then_inc(s_T3, 1)

            def router(g):
                pe.wait_ge(s_xT3, g + 1)
                x_h = xT3[:, :].rearrange("p (i x t) -> p i x t", i=TPG, x=2)
                for half in range(2):
                    last = nc.tensor.matmul(PT[L * half:L * half + L, 0:KH], wr_rep[:, :], x_h[:, :, half, :],
                                            start=True, stop=True)
                last.then_inc(s_RT, 1)

            def ffn(g):
                pe.wait_ge(s_xT3, g + 1)
                pe.wait_ge(s_qT, upto(g + 2))
                for i in range(TPG):
                    last = nc.tensor.matmul(PB[:, E * i:E * i + E], xT3[:, P * i:P * i + P], wblk_s[:, :],
                                            start=True, stop=True)
                last.then_inc(s_FF, 1)

            pe.wait_ge(consts2, 10)

            def fill(n):
                a, b = n + 2, n + 1
                if has(a):
                    transpose_x(a)
                if has(b):
                    attend(b, 1, 0)
                    attend(b, 1, 1)
                if has(a):
                    project_qk(a)
                if has(b):
                    transpose_ctx(b)
                    transpose_o(b)
                if has(a):
                    project_v(a)
                if has(b):
                    gla_out(b)
                if has(a):
                    aug_weights(a)
                if has(b):
                    context_values(b)
                    context_keys(b)
                if has(a):
                    project_g(a)
                if has(b):
                    queries(b)
                if has(a):
                    scores(a, 0)
                if has(b):
                    queries2(b)
                if has(a):
                    scores(a, 1)
                    attend(a, 0, 0)
                    attend(a, 0, 1)

            def step(n):
                a, b, c = n + 2, n + 1, n - 1
                if has(n):
                    x_scores(n, 0)
                if has(a):
                    transpose_x(a)
                if has(c):
                    transpose_x2(c)
                if has(n):
                    less_max(n, 0)
                if has(c):
                    router(c)
                if has(b):
                    attend(b, 1, 0)
                    attend(b, 1, 1)
                if has(c):
                    ffn(c)
                if has(n):
                    x_scores(n, 1)
                if has(b):
                    transpose_ctx(b)
                if has(n):
                    x_attend(n, 0, 0)
                    less_max(n, 1)
                if has(a):
                    project_qk(a)
                if has(n):
                    x_attend(n, 0, 1)
                    x_scores(n, 2)
                    x_values(n, 0, 0)
                    x_attend(n, 1, 0)
                    less_max(n, 2)
                if has(b):
                    context_keys(b)
                if has(n):
                    x_attend(n, 1, 1)
                    x_values(n, 0, 1)
                if has(a):
                    project_v(a)
                if has(n):
                    x_scores(n, 3)
                    x_attend(n, 2, 0)
                if has(a):
                    project_g(a)
                if has(n):
                    x_values(n, 1, 0)
                    x_values(n, 1, 1)
                    less_max(n, 3)
                    x_attend(n, 2, 1)
                if has(b):
                    transpose_o(b)
                if has(n):
                    x_values(n, 2, 0)
                    x_attend(n, 3, 0)
                if has(a):
                    aug_weights(a)
                if has(n):
                    x_values(n, 2, 1)
                if has(b):
                    gla_out(b)
                if has(n):
                    x_attend(n, 3, 1)
                    x_values(n, 3, 0)
                    x_values(n, 3, 1)
                if has(b):
                    context_values(b)
                if has(n):
                    x_out(n)
                if has(a):
                    scores(a, 0)
                if has(n):
                    x_out2(n)
                if has(b):
                    queries(b)
                if has(a):
                    attend(a, 0, 0)
                    attend(a, 0, 1)
                if has(b):
                    queries2(b)
                if has(a):
                    scores(a, 1)

            def drain(n):
                c = n - 1
                if has(n):
                    x_scores(n, 0)
                if has(c):
                    transpose_x2(c)
                if has(n):
                    less_max(n, 0)
                if has(c):
                    router(c)
                if has(n):
                    x_scores(n, 1)
                if has(c):
                    ffn(c)
                if has(n):
                    x_attend(n, 0, 0)
                    less_max(n, 1)
                    x_values(n, 0, 0)
                    x_attend(n, 0, 1)
                    x_scores(n, 2)
                    x_attend(n, 1, 0)
                    x_values(n, 0, 1)
                    less_max(n, 2)
                    x_attend(n, 1, 1)
                    x_values(n, 1, 0)
                    x_scores(n, 3)
                    x_values(n, 1, 1)
                    x_attend(n, 2, 0)
                    less_max(n, 3)
                    x_attend(n, 2, 1)
                    x_values(n, 2, 0)
                    x_attend(n, 3, 0)
                    x_values(n, 2, 1)
                    x_attend(n, 3, 1)
                    x_values(n, 3, 0)
                    x_values(n, 3, 1)
                    x_out(n)
                    x_out2(n)







            steps(pe, fill, step, drain)

        @block.scalar
        def _(act):
            def a_features(g):
                act.wait_ge(s_xT, g + 1)
                act.wait_ge(s_conv, TAPS * g)
                nc.scalar.copy(xpad_v[:, :, TAPS - 1:PADL], cut(PA0, SEQ, L)).then_inc(s_xpad, 1)

            def a_context(g):
                act.wait_ge(s_CT, g + 1)
                act.wait_ge(s_VX, g)
                nc.scalar.copy(cT[:, :], PA1[:, :]).then_inc(s_cT, 1)

            def a_silu(g):
                act.wait_ge(s_conv, TAPS * (g + 1))
                nc.scalar.activation(th1[:, :], y[:, :], ACT.Tanh).then_inc(s_th1, 1)

            def a_keys(g):
                act.wait_ge(s_KX, g + 1)
                act.wait_ge(s_kbd2, g)
                nc.scalar.copy(kx[:, :], AT1).then_inc(s_kx, 1)

            def a_key_blocks(g):
                act.wait_ge(s_kx, g + 1)
                act.wait_ge(s_S, TPG * g)
                for j in range(XHG // 2):
                    last = nc.scalar.activation(k_bdv[:, j, :], kx[:, :], ACT.Copy, scale=head_of[:, j:j + 1])
                last.then_inc(s_kbd, 1)

            def a_qk(g):
                act.wait_ge(s_QK, g + 1)
                act.wait_ge(s_qkp, g)
                nc.scalar.copy(qk[:, :], PA0[:, :]).then_inc(s_qk, 1)

            def a_gates(g):
                act.wait_ge(s_Gt, g + 1)
                act.wait_ge(s_sg, g)
                nc.scalar.activation(gh[:, :], AT0, ACT.Identity, bias=bg_half[:, :], scale=0.5).then_inc(s_gh, 1)

            def a_v(g):
                act.wait_ge(s_V, g + 1)
                act.wait_ge(s_vbd, 64 * g)
                act.wait_ge(s_z, g)
                nc.scalar.copy(vt[:, :], PA1[:, :]).then_inc(s_vt, 1)

            def a_gate(g):
                act.wait_ge(s_gh, g + 1)
                nc.scalar.activation(tg[:, :], gh[:, :], ACT.Tanh).then_inc(s_tg, 1)

            def a_log(g):
                act.wait_ge(s_qk, g + 1)
                nc.scalar.activation(ab[:, :], kg_s, ACT.Abs).then_inc(s_ab, 1)
                act.wait_ge(s_ab, g + 1)
                nc.scalar.activation(ex[:, :], ab[:, :], ACT.Exp, scale=-1.0).then_inc(s_ex, 1)
                act.wait_ge(s_ex, g + 1)
                act.wait_ge(s_lsig, g)
                nc.scalar.activation(ln1p[:, :], ex[:, :], ACT.Ln, bias=1.0).then_inc(s_ln, 1)

            def a_decays(g):
                act.wait_ge(s_lsig, g + 1)
                nc.scalar.activation(decay[:, :], lsig[:, :], ACT.Exp, scale=1.0 / NORMALIZER).then_inc(s_decay, 1)
                act.wait_ge(s_dq, g + 1)
                nc.scalar.activation(e_q[:, :], dq[:, :], ACT.Exp, scale=1.0 / NORMALIZER).then_inc(s_eq, 1)
                nc.scalar.activation(e_k[:, :], dq[:, :], ACT.Exp, scale=-1.0 / NORMALIZER).then_inc(s_ek, 1)
                act.wait_ge(s_drc, g + 1)
                act.wait_ge(s_kc, TPG * g)
                nc.scalar.activation(e_r[:, :], drc[:, :], ACT.Exp, scale=1.0 / NORMALIZER).then_inc(s_er, 1)

            def a_aug(g):
                act.wait_ge(s_z, g + 1)
                act.wait_ge(s_o, g)
                nc.scalar.activation(tz[:, :], z[:, :], ACT.Tanh, scale=0.5).then_inc(s_tz, 1)

            def a_square(g):
                act.wait_ge(s_dev, g + 1)
                act.wait_ge(s_oss, g)
                nc.scalar.activation(sq1[:, :], dev[:, :], ACT.Square).then_inc(s_sq1, 1)

            def a_values(g):
                act.wait_ge(s_VX, g + 1)
                act.wait_ge(s_PV, 2 * TPG * g)
                for half in range(2):
                    rows = slice(L * half, L * half + L)
                    dst = v_x[rows, :].rearrange("p (b q u v) -> p b q u v", b=SEQ, q=PAIRS, u=2)[:, :, :, half, 0:XD]
                    src = S[rows, :].rearrange("p (b q u v) -> p b q u v", b=SEQ, q=PAIRS, u=2)[:, :, :, half, :]
                    last = nc.scalar.copy(dst, src)
                last.then_inc(s_vx, 1)

            def b_queries(g):
                act.wait_ge(s_T2, g + 1)
                nc.scalar.copy(xT2[:, :], PT[:, :]).then_inc(s_xT2, 1)

            def b_queries2(g):
                act.wait_ge(s_Q, g + 1)
                act.wait_ge(s_S, TPG * g)
                for r in range(RUNS):
                    rows = slice(RUN * r, RUN * r + RUN)
                    last = nc.scalar.activation(qT_v[rows, r, :], PB[rows, :], ACT.Copy, scale=float(XD) ** -0.5)
                last.then_inc(s_qT, 1)

            def b_exp(g, i):
                act.wait_ge(s_fold, TPG * g + i + 1)
                nc.scalar.activation(pr_v[:, i % 2, :], S[:, :], ACT.Exp).then_inc(s_exp, 1)

            def b_probs(g, i):
                act.wait_ge(s_PT, 2 * (TPG * g + i) + 2)
                act.wait_ge(s_PV, 2 * (TPG * g + i))
                nc.scalar.copy(prT[:, 512:1024], PT[:, :]).then_inc(s_prT, 1)

            def b_out(g):
                act.wait_ge(s_CX, g + 1)
                nc.scalar.copy(cxT[:, :], PT[:, :]).then_inc(s_cxT, 1)

            def b_ffn(g):
                act.wait_ge(s_T3, g + 1)
                nc.scalar.copy(xT3[:, :], PT[:, :]).then_inc(s_xT3, 1)

            def b_gelu(g):
                act.wait_ge(s_FF, g + 1)
                act.wait_ge(s_gl, g)
                nc.scalar.activation(yh[:, :], PB[:, :], ACT.Copy, scale=0.5).then_inc(s_yh, 1)
                act.wait_ge(s_yh, g + 1)
                nc.scalar.activation(ysq[:, :], yh[:, :], ACT.Square).then_inc(s_ysq, 1)

            def b_gelu2(g):
                act.wait_ge(s_yv, g + 1)
                nc.scalar.activation(yt[:, :], yv[:, :], ACT.Tanh).then_inc(s_yt, 1)

            act.wait_ge(consts, 9)
            act.wait_ge(borne, 1)
            for t in (at, v_x, v_bd, qT):
                nc.scalar.copy(t[:, :], bearer[:, 0:1].to_broadcast([P, t.shape[1]])).then_inc(zeros, 1)

            def fill(n):
                a, b = n + 2, n + 1
                if has(a):
                    a_features(a)
                    a_silu(a)
                    a_qk(a)
                if has(b):
                    a_square(b)
                    a_context(b)
                if has(a):
                    a_log(a)
                    a_decays(a)
                    a_v(a)
                if has(b):
                    a_keys(b)
                    a_values(b)
                if has(a):
                    a_gates(a)
                    a_gate(a)
                if has(b):
                    b_queries(b)
                    b_queries2(b)
                    a_key_blocks(b)
                if has(a):
                    a_aug(a)

            def step(n):
                a, b, c = n + 2, n + 1, n - 1
                if has(a):
                    a_features(a)
                if has(c):
                    b_ffn(c)
                if has(n):
                    b_exp(n, 0)
                if has(c):
                    b_gelu(c)
                if has(a):
                    a_silu(a)
                if has(b):
                    a_square(b)
                    a_context(b)
                if has(n):
                    b_exp(n, 1)
                if has(a):
                    a_qk(a)
                if has(n):
                    b_probs(n, 0)
                if has(a):
                    a_log(a)
                if has(n):
                    b_exp(n, 2)
                if has(a):
                    a_decays(a)
                if has(n):
                    b_probs(n, 1)
                if has(b):
                    a_keys(b)
                if has(a):
                    a_v(a)
                    a_gates(a)
                if has(c):
                    b_gelu2(c)
                if has(n):
                    b_exp(n, 3)
                    b_probs(n, 2)
                if has(b):
                    a_key_blocks(b)
                if has(n):
                    b_probs(n, 3)
                    b_out(n)
                if has(a):
                    a_gate(a)
                if has(b):
                    a_values(b)
                if has(a):
                    a_aug(a)
                if has(b):
                    b_queries(b)
                    b_queries2(b)

            def drain(n):
                c = n - 1
                if has(c):
                    b_ffn(c)
                if has(n):
                    b_exp(n, 0)
                if has(c):
                    b_gelu(c)
                if has(n):
                    b_exp(n, 1)
                    b_probs(n, 0)
                    b_exp(n, 2)
                    b_probs(n, 1)
                    b_exp(n, 3)
                    b_probs(n, 2)
                if has(c):
                    b_gelu2(c)
                if has(n):
                    b_probs(n, 3)
                    b_out(n)







            steps(act, fill, step, drain)

        @block.vector
        def _(dve):
            def stats(g, n, src, st, mv, s_st, s_mv, s_xn):
                dve.wait_ge(s_xn, g)
                stv = cut(st, TPG, 6)
                for i in range(TPG):
                    last = nc.vector.bn_stats(stv[:, i, :], src(i))
                last.then_inc(s_st, 1)
                dve.wait_ge(s_st, g + 1)
                bear(n)
                for i in range(TPG):
                    last = nc.vector.bn_aggr(mv[:, 2 * i:2 * i + 2], stv[:, i, :])
                last.then_inc(s_mv, 1)

            def a_stats(g):
                if isinstance(g, int) and g == 1:
                    dve.wait_ge(x_rest, 16)
                stats(g, 0, lambda i: x_all[:, bass.ds((TPG * g + i) * E, E)], st1, mv1, s_st1, s_mv1, s_xn1)

            def norm(g, s_rs, s_read, s_xn, mv, rs, dst):
                dve.wait_ge(s_rs, g + 1)
                dve.wait_ge(s_read, g)
                for i in range(TPG):
                    last = nc.vector.tensor_scalar(dst[:, E * i:E * i + E], x_all[:, bass.ds((TPG * g + i) * E, E)],
                                                   mv[:, 2 * i:2 * i + 1], rs[:, i:i + 1],
                                                   ALU.subtract, ALU.mult)
                last.then_inc(s_xn, 1)

            def a_norm(g):
                norm(g, s_rs1, s_xT, s_xn1, mv1, rs1, xn1)

            def b_norm2(g):
                norm(g, s_rs2, s_T2, s_xn2, mv2, rs2, xn2)

            def a_conv(g):
                yv_ = cut(y, SEQ, L)
                dve.wait_ge(s_xpad, g + 1)
                nc.vector.tensor_scalar(yv_, xpad_v[:, :, 0:L], conv_half[:, 0:1], None, ALU.mult).then_inc(s_conv, 1)
                for k in range(1, TAPS):
                    dve.wait_ge(s_conv, TAPS * g + k)
                    nc.vector.scalar_tensor_tensor(out=yv_, in0=xpad_v[:, :, k:k + L], scalar=conv_half[:, k:k + 1],
                                                   in1=yv_, op0=ALU.mult, op1=ALU.add).then_inc(s_conv, 1)

            def a_silu(g):
                dve.wait_ge(s_th1, g + 1)
                for read in (s_QK, s_V, s_Gt):
                    dve.wait_ge(read, g)
                nc.vector.scalar_tensor_tensor(out=xcT[:, :], in0=th1[:, :], scalar=1.0, in1=y[:, :],
                                               op0=ALU.add, op1=ALU.mult).then_inc(s_xc, 1)

            def a_gate(g):
                dve.wait_ge(s_tg, g + 1)
                dve.wait_ge(s_og, g)
                nc.vector.scalar_tensor_tensor(out=sg[:, :], in0=tg[:, :], scalar=1.0, in1=gh[:, :],
                                               op0=ALU.add, op1=ALU.mult).then_inc(s_sg, 1)

            def a_decays(g):
                dve.wait_ge(s_ln, g + 1)
                dve.wait_ge(s_decay, g)
                nc.vector.scalar_tensor_tensor(out=lsig[:, :], in0=kg_s, scalar=0.0, in1=ln1p[:, :],
                                               op0=ALU.min, op1=ALU.subtract).then_inc(s_lsig, 1)
                dve.wait_ge(s_lsig, g + 1)
                nc.vector.tensor_scalar(lclip[:, :], lsig[:, :], LEAST_LOG, None, ALU.max).then_inc(s_lclip, 1)
                dve.wait_ge(s_lclip, g + 1)
                nc.vector.tensor_tensor_scan(G[:, :], carry[:, :], lclip[:, :], 0.0, ALU.mult, ALU.add).then_inc(s_G, 1)
                dve.wait_ge(s_G, g + 1)
                Gv = cut(G, TPG * NCH, CH)
                ref = cut(G, TPG, NCH, CH)[:, :, :, REF]
                dve.wait_ge(s_ek, g)
                nc.vector.tensor_tensor(cut(dq, TPG * NCH, CH), Gv,
                                        Gv[:, :, REF:REF + 1].to_broadcast([P, TPG * NCH, CH]),
                                        ALU.subtract).then_inc(s_dq, 1)
                nc.vector.tensor_tensor(cut(dr, TPG, NCH, NCH), ref.unsqueeze(3).to_broadcast([P, TPG, NCH, NCH]),
                                        ref.unsqueeze(2).to_broadcast([P, TPG, NCH, NCH]),
                                        ALU.subtract).then_inc(s_dr, 1)
                dve.wait_ge(s_dr, g + 1)
                dve.wait_ge(s_er, g)
                nc.vector.tensor_scalar(drc[:, :], dr[:, :], 0.0, None, ALU.min).then_inc(s_drc, 1)

            def a_keys(g):
                dve.wait_ge(s_decay, g + 1)
                nc.vector.tensor_scalar(key[:, :], decay[:, :], -1.0, 1.0, ALU.mult, ALU.add).then_inc(s_key, 1)
                dve.wait_ge(s_key, g + 1)
                dve.wait_ge(s_AUG, g)
                nc.vector.tensor_tensor(qkp[:, :], q_s, key[:, :], ALU.mult).then_inc(s_qkp, 1)

            def a_scaled_q(g):
                dve.wait_ge(s_eq, g + 1)
                dve.wait_ge(s_qbd, 16 * NB * g)
                nc.vector.scalar_tensor_tensor(out=qs[:, :], in0=q_s, scalar=float(DKH) ** -0.5, in1=e_q[:, :],
                                               op0=ALU.mult, op1=ALU.mult).then_inc(s_qs, 1)

            def a_scaled_k(g):
                dve.wait_ge(s_key, g + 1)
                dve.wait_ge(s_ek, g + 1)
                dve.wait_ge(s_kc, TPG * g)
                nc.vector.tensor_tensor(ke[:, :], key[:, :], e_k[:, :], ALU.mult).then_inc(s_ke, 1)

            def a_mask(g, j):
                dve.wait_ge(s_AT, 2 * g + j + 1)
                dve.wait_ge(s_AV, 2 * g)
                bear(3 + j)
                mask = cut(causal, NCH, CH).unsqueeze(2).to_broadcast([P, NCH, NB, CH])
                nc.vector.copy_predicated(at_c[:, j, :, :, :], mask, cut(AT, NCH, NB, CH)).then_inc(s_at, 1)

            def a_aug(g):
                dve.wait_ge(s_AUG, g + 1)
                dve.wait_ge(s_vt, g + 1)
                dve.wait_ge(s_tz, g)
                nc.vector.tensor_tensor(cut(z, TPG * H, DVH),
                                        PA0[:, 0:TPG * H].unsqueeze(2).to_broadcast([P, TPG * H, DVH]),
                                        cut(vt, TPG * H, DVH), ALU.mult).then_inc(s_z, 1)

            def a_center(g):
                dve.wait_ge(s_tz, g + 1)
                dve.wait_ge(s_AV, 2 * g + 2)
                nc.vector.scalar_tensor_tensor(out=o_s[:, :], in0=tz[:, :], scalar=0.5, in1=PA1[:, :],
                                               op0=ALU.mult, op1=ALU.add).then_inc(s_o, 1)
                dve.wait_ge(s_o, g + 1)
                nc.vector.tensor_reduce(osum[:, :], cut(o_s, TPG * H, DVH), AX.X, ALU.add).then_inc(s_osum, 1)
                dve.wait_ge(s_osum, g + 1)
                nc.vector.tensor_scalar(omean[:, :], osum[:, :], 1.0 / DVH, None, ALU.mult).then_inc(s_omean, 1)
                dve.wait_ge(s_omean, g + 1)
                dve.wait_ge(s_on, g)
                nc.vector.tensor_tensor(cut(dev, TPG * H, DVH), cut(o_s, TPG * H, DVH),
                                        omean[:, :].unsqueeze(2).to_broadcast([P, TPG * H, DVH]),
                                        ALU.subtract).then_inc(s_dev, 1)

            def a_squares(g):
                dve.wait_ge(s_sq1, g + 1)
                nc.vector.tensor_reduce(oss[:, :], cut(sq1, TPG * H, DVH), AX.X, ALU.add).then_inc(s_oss, 1)
                dve.wait_ge(s_oss, g + 1)
                dve.wait_ge(s_ors, g)
                nc.vector.tensor_scalar(ove[:, :], oss[:, :], 1.0 / DVH, EPS, ALU.mult, ALU.add).then_inc(s_ove, 1)

            def a_gated(g):
                dve.wait_ge(s_OT, g + 1)
                dve.wait_ge(s_sg, g + 1)
                dve.wait_ge(s_Y, g)
                nc.vector.tensor_tensor(ogT[:, :], PA0[:, :], sg[:, :], ALU.mult).then_inc(s_og, 1)

            def a_residual(g):
                dve.wait_ge(s_Y, g + 1)
                at_g = x_all[:, bass.ds(g * GT, GT)]
                nc.vector.tensor_tensor(at_g, PA1[:, :], at_g, ALU.add).then_inc(s_x1, 1)

            def b_stats2(g):
                dve.wait_ge(s_x1, g + 1)
                stats(g, 1, lambda i: x_all[:, bass.ds((TPG * g + i) * E, E)], st2, mv2, s_st2, s_mv2, s_xn2)

            def b_max(g, i):
                dve.wait_ge(s_S, TPG * g + i + 1)
                dve.wait_ge(s_fold, TPG * g + i)
                nc.vector.tensor_reduce(nmax[:, :], cut(S, XH, L), AX.X, ALU.max, negate=True).then_inc(s_max, 1)

            def b_probs(g, i):
                dve.wait_ge(s_PT, 2 * (TPG * g + i) + 1)
                if not isinstance(g, int) or TPG * g + i > 0:
                    dve.wait_ge(s_PV, 2 * (TPG * g + i) - 1)
                nc.vector.tensor_copy(prT[:, 0:512], PT[:, :]).then_inc(s_prT, 1)

            def b_weigh(g, i):
                dve.wait_ge(s_PV, 2 * (TPG * g + i) + 2)
                pv = PB[:, 0:XH * VC].rearrange("p (h v) -> p h v", h=XH)
                nc.vector.reciprocal(rden[:, :].unsqueeze(2), pv[:, :, XD:VC]).then_inc(s_rden, 1)
                dve.wait_ge(s_rden, TPG * g + i + 1)
                if i == 0:
                    dve.wait_ge(s_CX, g)
                nc.vector.tensor_tensor(cx[:, E * i:E * i + E].rearrange("p (h v) -> p h v", h=XH), pv[:, :, 0:XD],
                                        rden[:, :].unsqueeze(2).to_broadcast([P, XH, XD]),
                                        ALU.mult).then_inc(s_cx, 1)

            def b_residual(g):
                dve.wait_ge(s_WO, g + 1)
                dve.wait_ge(s_yout, g)
                nc.vector.tensor_tensor(x2[:, :], PB[:, :], x_all[:, bass.ds(g * GT, GT)], ALU.add).then_inc(s_x2, 1)
                dve.wait_ge(s_x2, g + 1)
                stats(g, 2, lambda i: x2[:, E * i:E * i + E], st3, mv3, s_st3, s_mv3, s_xn3)

            def b_route(g):
                dve.wait_ge(s_RT, g + 1)
                dve.wait_ge(s_own, g)
                nc.vector.tensor_copy(rs_all[:, :], PT[:, 0:KH]).then_inc(s_rall, 1)

            def b_own(g):
                dve.wait_ge(s_own, g + 1)
                nc.vector.tensor_reduce(r_own[:, :], cut(own, TPG, L), AX.X, ALU.add).then_inc(s_rown, 1)
                alls = cut(rs_all, TPG, L)
                mine = r_own[:, :].unsqueeze(2).to_broadcast([P, TPG, L])
                dve.wait_ge(s_rown, g + 1)
                dve.wait_ge(s_cnt, g)
                nc.vector.tensor_tensor(cut(above, TPG, L), alls, mine, ALU.is_gt).then_inc(s_above, 1)
                nc.vector.tensor_tensor(cut(tied, TPG, L), alls, mine, ALU.is_equal).then_inc(s_tied, 1)

            def b_taken(g):
                dve.wait_ge(s_cnt, g + 1)
                nc.vector.tensor_reduce(rank[:, :], cut(cnt, TPG, L), AX.X, ALU.add).then_inc(s_rank, 1)
                dve.wait_ge(s_rank, g + 1)
                nc.vector.tensor_scalar(taken[:, :], rank[:, :], float(KEEP), None, ALU.is_lt).then_inc(s_taken, 1)

            def b_gelu(g):
                dve.wait_ge(s_ysq, g + 1)
                nc.vector.tensor_scalar(yu[:, :], ysq[:, :], 8.0 * GELU_A * GELU_C, 2.0 * GELU_C, ALU.mult,
                                        ALU.add).then_inc(s_yu, 1)
                dve.wait_ge(s_yu, g + 1)
                nc.vector.tensor_tensor(yv[:, :], yu[:, :], yh[:, :], ALU.mult).then_inc(s_yv, 1)

            def b_result(g, part):
                if part == 0:
                    dve.wait_ge(s_yt, g + 1)
                    nc.vector.scalar_tensor_tensor(out=gl[:, :], in0=yt[:, :], scalar=1.0, in1=yh[:, :],
                                                   op0=ALU.add, op1=ALU.mult).then_inc(s_gl, 1)
                    return
                dve.wait_ge(s_gl, g + 1)
                dve.wait_ge(s_taken, g + 1)
                dve.wait_ge(s_xn3, g + 1)
                bear(5)
                take = taken[:, :].bitcast(u32).unsqueeze(2).to_broadcast([P, TPG, E])
                nc.vector.copy_predicated(cut(xn3, TPG, E), take, cut(gl, TPG, E)).then_inc(s_sel, 1)

            nc.vector.memset(bearer[:, :], 0.0).then_inc(borne, 1)
            dve.wait_ge(borne, 1)
            dve.wait_ge(x_in, 16)
            a_stats(0)
            a_norm(0)
            dve.wait_ge(w_in, 16 * len(WEIGHTS))
            dve.wait_ge(consts2, 10)
            nc.vector.tensor_scalar(conv_half[:, :], conv_s[:, :], 0.5, None, ALU.mult)
            nc.vector.tensor_scalar(bg_half[:, :], bg_s[:, :], 0.5, None, ALU.mult)
            nc.vector.tensor_copy(causal[:, :], causal_f[:, :])
            nc.vector.tensor_scalar(aug_sel[:, :], block_of[:, :], aug_s[:, 0:1], None, ALU.mult)
            nc.vector.tensor_reduce(head_of[:, :], block_of[:, :].rearrange("p (r j) -> p j r", r=RUNS), AX.X, ALU.add)
            nc.vector.tensor_copy(ident_b[:, :], ident[:, :])
            nc.vector.tensor_copy(wr_rep[:, :], wr_s[:, 0:1].to_broadcast([P, L])).then_inc(derived, 1)
            dve.wait_ge(derived, 1)
            dve.wait_ge(zeros, 2)
            for half in range(2):
                ones = v_x[L * half:L * half + L, :].rearrange("p (b q u v) -> p b q u v", b=SEQ, q=PAIRS, u=2)
                nc.vector.memset(ones[:, :, :, half, XD:VC].rearrange("p b q v -> p (b q) v"), 1.0)

            def fill(n):
                a, b = n + 2, n + 1
                if has(a):
                    a_conv(a)
                    a_silu(a)
                if has(b):
                    a_center(b)
                    a_squares(b)
                if has(a):
                    a_decays(a)
                    a_scaled_q(a)
                    a_keys(a)
                if has(a + 1):
                    a_stats(a + 1)
                if has(b):
                    a_gated(b)
                if has(a):
                    a_scaled_k(a)
                if has(b):
                    a_residual(b)
                    b_stats2(b)
                if has(a + 1):
                    a_norm(a + 1)
                if has(b):
                    b_norm2(b)
                if has(a):
                    a_mask(a, 0)
                    a_gate(a)
                    a_aug(a)
                    a_mask(a, 1)

            def step(n):
                a, b, c = n + 2, n + 1, n - 1
                if has(n):
                    b_max(n, 0)
                if has(a):
                    a_conv(a)
                if has(c):
                    b_route(c)
                if has(b):
                    a_center(b)
                if has(n):
                    b_max(n, 1)
                if has(a):
                    a_silu(a)
                if has(n):
                    b_probs(n, 0)
                if has(b):
                    a_squares(b)
                if has(c):
                    b_own(c)
                if has(n):
                    b_max(n, 2)
                    b_probs(n, 1)
                if has(c):
                    b_gelu(c)
                if has(a):
                    a_decays(a)
                    a_scaled_q(a)
                if has(n):
                    b_weigh(n, 0)
                    b_max(n, 3)
                if has(a):
                    a_keys(a)
                if has(n):
                    b_probs(n, 2)
                if has(a):
                    a_scaled_k(a)
                if has(n):
                    b_weigh(n, 1)
                if has(b):
                    a_gated(b)
                if has(c):
                    b_taken(c)
                    b_result(c, 0)
                if has(n):
                    b_probs(n, 3)
                    b_weigh(n, 2)
                if has(b):
                    a_residual(b)
                    b_stats2(b)
                if has(c):
                    b_result(c, 1)
                if has(n):
                    b_weigh(n, 3)
                if has(a):
                    a_aug(a)
                if has(a + 1):
                    a_stats(a + 1)
                if has(b):
                    b_norm2(b)
                if has(a):
                    a_mask(a, 0)
                if has(n):
                    b_residual(n)
                if has(a):
                    a_gate(a)
                if has(a + 1):
                    a_norm(a + 1)
                if has(a):
                    a_mask(a, 1)

            def drain(n):
                c = n - 1
                if has(n):
                    b_max(n, 0)
                if has(c):
                    b_route(c)
                if has(n):
                    b_max(n, 1)
                    b_probs(n, 0)
                if has(c):
                    b_own(c)
                if has(n):
                    b_max(n, 2)
                    b_probs(n, 1)
                    b_weigh(n, 0)
                if has(c):
                    b_gelu(c)
                if has(n):
                    b_max(n, 3)
                    b_probs(n, 2)
                    b_weigh(n, 1)
                    b_probs(n, 3)
                    b_weigh(n, 2)
                if has(c):
                    b_taken(c)
                    b_result(c, 0)
                if has(n):
                    b_weigh(n, 3)
                if has(c):
                    b_result(c, 1)
                if has(n):
                    b_residual(n)







            steps(dve, fill, step, drain)


_SHAPE = (64, 64, 128)


def kernel(x, ctx_1024, mask_1_bf0, L0_attn_conv_w, L0_attn_wq, L0_attn_wkg, L0_attn_wv, L0_attn_wg, L0_attn_bg,
           L0_attn_wout, L0_attn_aug_balance, L0_xattn_Wq, L0_xattn_Wk, L0_xattn_Wv, L0_xattn_Wo,
           L0_ffn_w_router, L0_ffn_w_block):
    import numpy as np
    import concourse.bacc as bacc
    from concourse.bass_utils import run_bass_kernel_spmd

    ins = {
        "x": x, "ctx": ctx_1024, "conv_w": L0_attn_conv_w, "wq": L0_attn_wq, "wkg": L0_attn_wkg,
        "wv": L0_attn_wv, "wg": L0_attn_wg, "bg": np.asarray(L0_attn_bg)[:, None], "wout": L0_attn_wout,
        "aug": np.asarray(L0_attn_aug_balance)[:, None], "WqT": np.asarray(L0_xattn_Wq).T,
        "WkT": np.asarray(L0_xattn_Wk).T, "WvT": np.asarray(L0_xattn_Wv).T, "WoT": np.asarray(L0_xattn_Wo).T,
        "w_router": np.asarray(L0_ffn_w_router)[:, None], "w_block": L0_ffn_w_block,
    }
    nc = bacc.Bacc("TRN2", target_bir_lowering=False, num_devices=1)
    arrays, args = {}, []
    for name, a in ins.items():
        a = np.ascontiguousarray(a)
        arrays[f"in_{name}"] = a
        args.append(nc.dram_tensor(f"in_{name}", a.shape, mybir.dt.from_np(a.dtype), kind="ExternalInput").ap())
    args.append(nc.dram_tensor("out_0", _SHAPE, mybir.dt.float32, kind="ExternalOutput").ap())
    decoder_layer(nc, *args)
    r = run_bass_kernel_spmd(nc, [arrays], core_ids=[0])
    return r.results[0]["out_0"]
```
